# Optimizing a Trainium2 kernel written in Bass

```python
import numpy as np
import jax
import jax.numpy as jnp

def _softmax(x, axis=-1):
    return jax.nn.softmax(x, axis=axis)

def _gelu(x):
    return jax.nn.gelu(x, approximate=True)

def _silu(x):
    return jax.nn.silu(x)

def _sigmoid(x):
    return jax.nn.sigmoid(x)

def _layernorm(x, axis=-1, eps=1e-05):
    m = jnp.mean(x, axis=axis, keepdims=True)
    v = jnp.var(x, axis=axis, keepdims=True)
    return (x - m) / jnp.sqrt(v + eps)

def _scatter_add(tgt, idx, src, axis=0):
    return tgt.at[idx].add(src)

def _segment_sum(src, seg, n):
    return jax.ops.segment_sum(src, seg, n)
kernel_name = 'mk_flamingo_gated_d2_seqx_r8_671cfb'

def setup_inputs(seed: int=0):
    np.random.seed(seed)
    _w = jnp.asarray

    def _rec_inputs():
        import jax
        import jax.numpy as jnp
        _rk = jax.random.key(seed)
        x = -0.0003929 + 0.9999 * jax.random.normal(jax.random.fold_in(_rk, 1), (1, 1024, 128), jnp.float32)
        _lenS = 1024 - jax.random.randint(jax.random.fold_in(_rk, 7), (1,), 0, max(1, 1024 // 4) + 1, jnp.int32)
        _lenS2 = 6404 - jax.random.randint(jax.random.fold_in(_rk, 8), (1,), 0, max(1, 6404 // 4) + 1, jnp.int32)
        _ctx_768P = jax.random.normal(jax.random.fold_in(_rk, 11), (1, 16, 96), jnp.float32)
        _ctx_768c = jax.random.dirichlet(jax.random.fold_in(_rk, 511), 0.3 * jnp.ones((16,), jnp.float32), (1, 6404))
        _ctx_768t = jnp.einsum('bsk,bkd->bsd', _ctx_768c, _ctx_768P)
        _ctx_768t = _ctx_768t * jax.lax.rsqrt(jnp.mean(jnp.square(_ctx_768t)) + 1e-12) * 0.953939
        ctx_768 = 0.00095986 + 0.999812 * (_ctx_768t + 0.3 * jax.random.normal(jax.random.fold_in(_rk, 611), (1, 6404, 96), jnp.float32))
        _validS = jnp.arange(1024)[None, :] < _lenS[:, None]
        _validS2 = jnp.arange(6404)[None, :] < _lenS2[:, None]
        _causal = jnp.tril(jnp.ones((1024, 1024), dtype=bool))
        mask_BxS2_bf1 = jnp.ones((1, 6404), dtype=bool)
        mask_BxS2_bk0 = jnp.logical_not(jnp.broadcast_to(_validS2[:, :], (1, 6404)))
        _g = jax.random.normal(jax.random.fold_in(_rk, 9001), (2, 2), jnp.float32)
        _g = jnp.sign(_g) * jnp.maximum(jnp.abs(_g), 1.0) + (_g == 0) * 1.0
        g_xattn = _g[0]
        g_ffn = _g[1]
        return (x, ctx_768, mask_BxS2_bf1, mask_BxS2_bk0, g_xattn, g_ffn)
    x, ctx_768, mask_BxS2_bf1, mask_BxS2_bk0, g_xattn, g_ffn = _rec_inputs()

    def _L0_xattn_setup():
        import jax, jax.numpy as jnp
        import numpy as np
        DIM = 128
        CTX_DIM = 96
        HEADS = 16
        key = jax.random.key(seed)
        ks = jax.random.split(key, 7)
        B, N, M = (4, 512, 32)
        x = jax.random.normal(ks[0], (B, N, DIM), dtype=jnp.float32)
        context = jax.random.normal(ks[1], (B, M, CTX_DIM), dtype=jnp.float32)
        context_mask = jnp.ones((B, M), dtype=bool)
        s_d = 1.0 / np.sqrt(DIM)
        s_c = 1.0 / np.sqrt(CTX_DIM)
        Wq = jax.random.normal(ks[2], (DIM, DIM), dtype=jnp.float32) * s_d
        Wk = jax.random.normal(ks[3], (CTX_DIM, DIM), dtype=jnp.float32) * s_c
        Wv = jax.random.normal(ks[4], (CTX_DIM, DIM), dtype=jnp.float32) * s_c
        Wo = jax.random.normal(ks[5], (DIM, DIM), dtype=jnp.float32) * s_d
        return {'x': x, 'context': context, 'context_mask': context_mask, 'Wq': Wq, 'Wk': Wk, 'Wv': Wv, 'Wo': Wo}
    _L0_xattn_all = _L0_xattn_setup()
    _L0_xattn_in = {k: v for k, v in _L0_xattn_all.items() if k in ('Wq', 'Wk', 'Wv', 'Wo')}
    del _L0_xattn_all

    def _L0_ffn_setup():
        import jax, jax.numpy as jnp
        import numpy as np
        B, S, D, E, F, TOP_K = (4, 256, 128, 8, 512, 2)
        key = jax.random.key(seed)
        k0, k1, k2, k3 = jax.random.split(key, 4)
        init = lambda k, shape, fan: (jax.random.normal(k, shape, jnp.float32) / np.sqrt(fan)).astype(jnp.float32)
        return {'x': jax.random.normal(k0, (B, S, D), jnp.float32), 'gate_w': init(k1, (D, E), D), 'w1': init(k2, (E, D, F), D), 'b1': jnp.zeros((E, F), jnp.float32), 'w2': init(k3, (E, F, D), F), 'b2': jnp.zeros((E, D), jnp.float32)}
    _L0_ffn_all = _L0_ffn_setup()
    _L0_ffn_in = {k: v for k, v in _L0_ffn_all.items() if k in ('gate_w', 'w1', 'b1', 'w2', 'b2')}
    del _L0_ffn_all

    def _L1_xattn_setup():
        import jax, jax.numpy as jnp
        import numpy as np
        HEADS = 8
        DIM_HEAD = 64
        QUERY_DIM = 128
        CONTEXT_DIM = 96
        INNER = HEADS * DIM_HEAD
        key = jax.random.key(seed)
        ks = jax.random.split(key, 8)
        b, n, j = (4, 256, 256)
        x = jax.random.normal(ks[0], (b, n, QUERY_DIM), dtype=jnp.float32)
        context = jax.random.normal(ks[1], (b, j, CONTEXT_DIM), dtype=jnp.float32)
        mask = jax.random.randint(ks[2], (b, j), 0, 2).astype(jnp.bool_)
        W_q = jax.random.normal(ks[3], (QUERY_DIM, INNER), dtype=jnp.float32) / np.sqrt(QUERY_DIM)
        W_k = jax.random.normal(ks[4], (CONTEXT_DIM, INNER), dtype=jnp.float32) / np.sqrt(CONTEXT_DIM)
        W_v = jax.random.normal(ks[5], (CONTEXT_DIM, INNER), dtype=jnp.float32) / np.sqrt(CONTEXT_DIM)
        W_o = jax.random.normal(ks[6], (INNER, QUERY_DIM), dtype=jnp.float32) / np.sqrt(INNER)
        b_o = jax.random.normal(ks[7], (QUERY_DIM,), dtype=jnp.float32) * 0.01
        return {'x': x, 'context': context, 'mask': mask, 'W_q': W_q, 'W_k': W_k, 'W_v': W_v, 'W_o': W_o, 'b_o': b_o}
    _L1_xattn_all = _L1_xattn_setup()
    _L1_xattn_in = {k: v for k, v in _L1_xattn_all.items() if k in ('W_q', 'W_k', 'W_v', 'W_o', 'b_o')}
    del _L1_xattn_all

    def _L1_ffn_setup():
        import jax, jax.numpy as jnp
        import numpy as np
        import math
        B, S, D = (2, 256, 128)
        H = 16
        HD = D // H
        FFN = 256
        E = 8
        TOP_K = 2
        CAP_FACTOR = 1.25
        EPS = 1e-06
        BASE = 10000.0
        CAP = max(math.ceil(B * S * TOP_K * CAP_FACTOR / E), 1)

        def _rmsnorm(x, w):
            rms = jax.lax.rsqrt(jnp.mean(x * x, axis=-1, keepdims=True) + EPS)
            return w * x * rms

        def _rope(x, cos, sin):
            xr = x[..., 0::2]
            xi = x[..., 1::2]
            c = cos[None, None]
            s_ = sin[None, None]
            out_r = xr * c - xi * s_
            out_i = xr * s_ + xi * c
            return jnp.stack([out_r, out_i], axis=-1).reshape(x.shape)

        def _mha(x, w_qkv, w_o):
            b, s, d = x.shape
            qkv = x @ w_qkv
            q, k, v = jnp.split(qkv, 3, axis=-1)
            to_heads = lambda z: z.reshape(b, s, H, HD).transpose(0, 2, 1, 3)
            q, k, v = (to_heads(q), to_heads(k), to_heads(v))
            theta = BASE ** (-2.0 * (jnp.arange(HD // 2, dtype=jnp.float32) / HD))
            freqs = jnp.arange(s, dtype=jnp.float32)[:, None] * theta[None, :]
            cos, sin = (jnp.cos(freqs), jnp.sin(freqs))
            q = _rope(q, cos, sin)
            k = _rope(k, cos, sin)
            scores = jnp.einsum('bhqd,bhkd->bhqk', q, k) / jnp.sqrt(jnp.float32(HD))
            causal = jnp.tril(jnp.ones((s, s), dtype=bool))
            scores = jnp.where(causal, scores, -jnp.inf)
            attn = jax.nn.softmax(scores, axis=-1)
            y = jnp.einsum('bhqk,bhkd->bhqd', attn, v)
            y = y.transpose(0, 2, 1, 3).reshape(b, s, d)
            return y @ w_o

        def _moe(x, w_router, w1, w2):
            b, s, d = x.shape
            t = b * s
            xf = x.reshape(t, d)
            logits = xf.astype(jnp.float32) @ w_router.astype(jnp.float32)
            probs = jax.nn.softmax(logits, axis=-1)
            g, eidx = jax.lax.top_k(probs, TOP_K)
            fg = g.reshape(t * TOP_K)
            fe = eidx.reshape(t * TOP_K)
            tok_of = jnp.arange(t * TOP_K) // TOP_K
            masked = jnp.where(fe[None, :] == jnp.arange(E)[:, None], fg[None, :], -jnp.inf)
            vals, idx = jax.lax.top_k(masked, CAP)
            valid = jnp.isfinite(vals)
            gates = jnp.where(valid, vals, 0.0)
            tok = tok_of[idx]
            xe = xf[tok]
            h = jax.nn.relu(jnp.einsum('ecd,edf->ecf', xe, w1))
            ye = jnp.einsum('ecf,efd->ecd', h, w2) * gates[..., None]
            y = jnp.zeros_like(xf).at[tok.reshape(-1)].add(ye.reshape(-1, d))
            return y.reshape(b, s, d)
        key = jax.random.key(seed)
        ks = jax.random.split(key, 6)
        sd = 0.02
        return {'x': jax.random.normal(ks[0], (B, S, D), jnp.float32), 'g1': jnp.ones((D,), jnp.float32), 'w_qkv': jax.random.normal(ks[1], (D, 3 * D), jnp.float32) * sd, 'w_o': jax.random.normal(ks[2], (D, D), jnp.float32) * sd, 'g2': jnp.ones((D,), jnp.float32), 'w_router': jax.random.normal(ks[3], (D, E), jnp.float32) * sd, 'w1': jax.random.normal(ks[4], (E, D, FFN), jnp.float32) * sd, 'w2': jax.random.normal(ks[5], (E, FFN, D), jnp.float32) * sd}
    _L1_ffn_all = _L1_ffn_setup()
    _L1_ffn_in = {k: v for k, v in _L1_ffn_all.items() if k in ('g1', 'w_qkv', 'w_o', 'g2', 'w_router', 'w1', 'w2')}
    del _L1_ffn_all
    return {'x': x, 'ctx_768': ctx_768, 'mask_BxS2_bf1': mask_BxS2_bf1, 'mask_BxS2_bk0': mask_BxS2_bk0, 'g_xattn': g_xattn, 'g_ffn': g_ffn, 'L0_xattn_Wq': _L0_xattn_in['Wq'], 'L0_xattn_Wk': _L0_xattn_in['Wk'], 'L0_xattn_Wv': _L0_xattn_in['Wv'], 'L0_xattn_Wo': _L0_xattn_in['Wo'], 'L0_ffn_gate_w': _L0_ffn_in['gate_w'], 'L0_ffn_w1': _L0_ffn_in['w1'], 'L0_ffn_b1': _L0_ffn_in['b1'], 'L0_ffn_w2': _L0_ffn_in['w2'], 'L0_ffn_b2': _L0_ffn_in['b2'], 'L1_xattn_W_q': _L1_xattn_in['W_q'], 'L1_xattn_W_k': _L1_xattn_in['W_k'], 'L1_xattn_W_v': _L1_xattn_in['W_v'], 'L1_xattn_W_o': _L1_xattn_in['W_o'], 'L1_xattn_b_o': _L1_xattn_in['b_o'], 'L1_ffn_g1': _L1_ffn_in['g1'], 'L1_ffn_w_qkv': _L1_ffn_in['w_qkv'], 'L1_ffn_w_o': _L1_ffn_in['w_o'], 'L1_ffn_g2': _L1_ffn_in['g2'], 'L1_ffn_w_router': _L1_ffn_in['w_router'], 'L1_ffn_w1': _L1_ffn_in['w1'], 'L1_ffn_w2': _L1_ffn_in['w2']}

def reference(x, ctx_768, mask_BxS2_bf1, mask_BxS2_bk0, g_xattn, g_ffn, L0_xattn_Wq, L0_xattn_Wk, L0_xattn_Wv, L0_xattn_Wo, L0_ffn_gate_w, L0_ffn_w1, L0_ffn_b1, L0_ffn_w2, L0_ffn_b2, L1_xattn_W_q, L1_xattn_W_k, L1_xattn_W_v, L1_xattn_W_o, L1_xattn_b_o, L1_ffn_g1, L1_ffn_w_qkv, L1_ffn_w_o, L1_ffn_g2, L1_ffn_w_router, L1_ffn_w1, L1_ffn_w2):
    import jax
    import jax.numpy as jnp

    def _L0_xattn_ref(x, context, context_mask, Wq, Wk, Wv, Wo):
        import jax, jax.numpy as jnp
        import numpy as np
        DIM = 128
        CTX_DIM = 96
        HEADS = 16
        B, N, _ = x.shape
        M = context.shape[1]
        hd = DIM // HEADS
        scale = hd ** (-0.5)
        q = (x @ Wq).reshape(B, N, HEADS, hd).transpose(0, 2, 1, 3)
        k = (context @ Wk).reshape(B, M, HEADS, hd).transpose(0, 2, 1, 3)
        v = (context @ Wv).reshape(B, M, HEADS, hd).transpose(0, 2, 1, 3)
        scores = jnp.einsum('bhid,bhjd->bhij', q, k) * scale
        max_neg = -jnp.finfo(scores.dtype).max
        scores = jnp.where(context_mask[:, None, None, :], scores, max_neg)
        attn = jax.nn.softmax(scores, axis=-1)
        out = jnp.einsum('bhij,bhjd->bhid', attn, v)
        out = out.transpose(0, 2, 1, 3).reshape(B, N, DIM)
        return out @ Wo

    def _L0_ffn_ref(x, gate_w, w1, b1, w2, b2):
        import jax, jax.numpy as jnp
        import numpy as np
        B, S, D, E, F, TOP_K = (4, 256, 128, 8, 512, 2)
        b, s, d = x.shape
        e = gate_w.shape[1]
        xf = x.reshape(-1, d)
        t = xf.shape[0]
        logits = xf @ gate_w
        top_w, top_idx = jax.lax.top_k(logits, TOP_K)
        top_w = jax.nn.softmax(top_w.astype(jnp.float32), axis=-1).astype(x.dtype)
        combine = jnp.zeros((t, e), x.dtype).at[jnp.arange(t)[:, None], top_idx].add(top_w)
        h = jax.nn.gelu(jnp.einsum('td,edf->tef', xf, w1) + b1, approximate=False)
        y = jnp.einsum('tef,efd->ted', h, w2) + b2
        out = jnp.einsum('ted,te->td', y, combine)
        return out.reshape(b, s, d)

    def _L1_xattn_ref(x, context, mask, W_q, W_k, W_v, W_o, b_o):
        import jax, jax.numpy as jnp
        import numpy as np
        HEADS = 8
        DIM_HEAD = 64
        QUERY_DIM = 128
        CONTEXT_DIM = 96
        INNER = HEADS * DIM_HEAD
        b, n, _ = x.shape
        j = context.shape[1]
        scale = DIM_HEAD ** (-0.5)
        q = (x @ W_q).reshape(b, n, HEADS, DIM_HEAD)
        k = (context @ W_k).reshape(b, j, HEADS, DIM_HEAD)
        v = (context @ W_v).reshape(b, j, HEADS, DIM_HEAD)
        sim = jnp.einsum('bihd,bjhd->bhij', q, k) * scale
        max_neg = -jnp.finfo(sim.dtype).max
        sim = jnp.where(mask[:, None, None, :], sim, max_neg)
        attn = jax.nn.softmax(sim, axis=-1)
        out = jnp.einsum('bhij,bjhd->bihd', attn, v).reshape(b, n, INNER)
        return out @ W_o + b_o

    def _L1_ffn_ref(x, g1, w_qkv, w_o, g2, w_router, w1, w2):
        import jax, jax.numpy as jnp
        import numpy as np
        import math
        B, S, D = (2, 256, 128)
        H = 16
        HD = D // H
        FFN = 256
        E = 8
        TOP_K = 2
        CAP_FACTOR = 1.25
        EPS = 1e-06
        BASE = 10000.0
        CAP = max(math.ceil(B * S * TOP_K * CAP_FACTOR / E), 1)

        def _rmsnorm(x, w):
            rms = jax.lax.rsqrt(jnp.mean(x * x, axis=-1, keepdims=True) + EPS)
            return w * x * rms

        def _rope(x, cos, sin):
            xr = x[..., 0::2]
            xi = x[..., 1::2]
            c = cos[None, None]
            s_ = sin[None, None]
            out_r = xr * c - xi * s_
            out_i = xr * s_ + xi * c
            return jnp.stack([out_r, out_i], axis=-1).reshape(x.shape)

        def _mha(x, w_qkv, w_o):
            b, s, d = x.shape
            qkv = x @ w_qkv
            q, k, v = jnp.split(qkv, 3, axis=-1)
            to_heads = lambda z: z.reshape(b, s, H, HD).transpose(0, 2, 1, 3)
            q, k, v = (to_heads(q), to_heads(k), to_heads(v))
            theta = BASE ** (-2.0 * (jnp.arange(HD // 2, dtype=jnp.float32) / HD))
            freqs = jnp.arange(s, dtype=jnp.float32)[:, None] * theta[None, :]
            cos, sin = (jnp.cos(freqs), jnp.sin(freqs))
            q = _rope(q, cos, sin)
            k = _rope(k, cos, sin)
            scores = jnp.einsum('bhqd,bhkd->bhqk', q, k) / jnp.sqrt(jnp.float32(HD))
            causal = jnp.tril(jnp.ones((s, s), dtype=bool))
            scores = jnp.where(causal, scores, -jnp.inf)
            attn = jax.nn.softmax(scores, axis=-1)
            y = jnp.einsum('bhqk,bhkd->bhqd', attn, v)
            y = y.transpose(0, 2, 1, 3).reshape(b, s, d)
            return y @ w_o

        def _moe(x, w_router, w1, w2):
            b, s, d = x.shape
            t = b * s
            xf = x.reshape(t, d)
            logits = xf.astype(jnp.float32) @ w_router.astype(jnp.float32)
            probs = jax.nn.softmax(logits, axis=-1)
            g, eidx = jax.lax.top_k(probs, TOP_K)
            fg = g.reshape(t * TOP_K)
            fe = eidx.reshape(t * TOP_K)
            tok_of = jnp.arange(t * TOP_K) // TOP_K
            masked = jnp.where(fe[None, :] == jnp.arange(E)[:, None], fg[None, :], -jnp.inf)
            vals, idx = jax.lax.top_k(masked, CAP)
            valid = jnp.isfinite(vals)
            gates = jnp.where(valid, vals, 0.0)
            tok = tok_of[idx]
            xe = xf[tok]
            h = jax.nn.relu(jnp.einsum('ecd,edf->ecf', xe, w1))
            ye = jnp.einsum('ecf,efd->ecd', h, w2) * gates[..., None]
            y = jnp.zeros_like(xf).at[tok.reshape(-1)].add(ye.reshape(-1, d))
            return y.reshape(b, s, d)
        x = x + _mha(_rmsnorm(x, g1), w_qkv, w_o)
        x = x + _moe(_rmsnorm(x, g2), w_router, w1, w2)
        return x
    x = x + jnp.tanh(g_xattn[0]) * _L0_xattn_ref(_layernorm(x, axis=-1), ctx_768, mask_BxS2_bf1, L0_xattn_Wq, L0_xattn_Wk, L0_xattn_Wv, L0_xattn_Wo)
    x = x + jnp.tanh(g_ffn[0]) * _L0_ffn_ref(_layernorm(x, axis=-1), L0_ffn_gate_w, L0_ffn_w1, L0_ffn_b1, L0_ffn_w2, L0_ffn_b2)
    x = x + jnp.tanh(g_xattn[1]) * _L1_xattn_ref(_layernorm(x, axis=-1), ctx_768, mask_BxS2_bk0, L1_xattn_W_q, L1_xattn_W_k, L1_xattn_W_v, L1_xattn_W_o, L1_xattn_b_o)
    x = x + jnp.tanh(g_ffn[1]) * _L1_ffn_ref(_layernorm(x, axis=-1), L1_ffn_g1, L1_ffn_w_qkv, L1_ffn_w_o, L1_ffn_g2, L1_ffn_w_router, L1_ffn_w1, L1_ffn_w2)
    return x

_drawn_inputs = setup_inputs


def setup_inputs(seed=0):
    import zlib

    import numpy as np

    out = dict(_drawn_inputs(seed))
    spreads = {'g_ffn': (-1.0, 0.2),
     'L0_ffn_b1': (0.0, 0.1),
     'L0_ffn_b2': (0.0, 0.1),
     'L1_ffn_g1': (1.0, 0.6),
     'L1_ffn_g2': (1.0, 0.6)}
    factors = {'L1_xattn_b_o': 7.292, 'L1_ffn_w_router': 3.868, 'L1_ffn_w1': 4.227, 'L1_ffn_w2': 3.533}
    for name, (base, spread) in spreads.items():
        noise = np.random.default_rng([zlib.crc32(name.encode()), seed]).standard_normal(out[name].shape)
        drawn = base * np.exp(spread * noise) if base else spread * noise
        out[name] = jnp.asarray(drawn.astype(out[name].dtype))
    for name, factor in factors.items():
        out[name] = (out[name] * factor).astype(out[name].dtype)
    return out
```

```python
from contextlib import ExitStack

import numpy as np

import concourse.bass as bass
from concourse import mybir

F32 = mybir.dt.float32
F32R = mybir.dt.float32r
BF16 = mybir.dt.bfloat16
U8 = mybir.dt.uint8
U32 = mybir.dt.uint32
ALU = mybir.AluOpType
ACT = mybir.ActivationFunctionType
AX = mybir.AxisListType
RMAX = bass.bass_isa.ReduceOp.max
ds = bass.ds

P = 128
N = 1024
D = 128
NT = N // P
HALF = 512
CTX = 6404
CD = 96
KT = -(-CTX // P)
KF = KT - 1
MID_TILE = KT // 2
TAIL = CTX - KF * P
BIG = 1.0e30
EPS_LN = 1e-5
EPS_RMS = 1e-6

H0 = 16
HD0 = D // H0
GH = 4
NG = H0 // GH
NU0 = 2 * NG
SPLIT = [(0, 0), (0, 1), (1, 0), (1, 1), (0, 2), (2, 0)]
ROWS = 2 + 16 * len(SPLIT)
VW = HD0 + 1

H1 = 8
HD1 = 64
CR = CD + 2

CH = 512
CHUNKS = [(c * CH, min(CH, CTX - c * CH)) for c in range(-(-CTX // CH))]
NC = len(CHUNKS)

PROB_RING0 = 4
PROB_RING = 3
SCORE_RING = 2
MAX_RING0 = 3
MAX_CREDIT = 6


def back_in_ring(n, per_unit, ring):
    if n >= ring:
        return ring
    return per_unit + n - max(k for k in range(per_unit) if k % ring == n)


def tiles_of(c):
    return [(t, P if t < KF else TAIL) for t in range(4 * c, min(4 * c + 4, KT))]


class Chain:

    def __init__(self, eng, sem):
        self.eng, self.sem, self.n = eng, sem, 0

    def link(self, ins):
        self.n += 1
        ins.then_inc(self.sem, 1)
        self.eng.wait_ge(self.sem, self.n)


class Mem:

    def __init__(self, nc):
        self.nc, self.stack, self.sems = nc, ExitStack(), []

    def sb(self, name, shape, dt=F32):
        return self.stack.enter_context(self.nc.sbuf_tensor(name, shape, dt))

    def ps(self, name, shape, dt=F32):
        return self.stack.enter_context(self.nc.psum_tensor(name, shape, dt))

    def sem(self, name):
        self.sems.append(self.stack.enter_context(self.nc.semaphore(name)))
        return self.sems[-1]

    def close(self):
        if self.sems:
            with self.nc.Block() as block:
                @block.sync
                def _(sp):
                    for sem in self.sems:
                        sp.sem_clear(sem)
        self.stack.close()


def norm_block(nc, tag, src, out_tok, out_T, ident, eps, gain=None):
    m = Mem(nc)
    stats = m.sb(f"{tag}_stats", [P, NT, 6])
    mv = m.sb(f"{tag}_mv", [P, NT, 2])
    ms = m.sb(f"{tag}_ms", [P, NT])
    var = m.sb(f"{tag}_var", [P, NT])
    std = m.sb(f"{tag}_std", [P, NT])
    rstd = m.sb(f"{tag}_rstd", [P, NT])
    scaled = m.sb(f"{tag}_scaled", [P, NT, D]) if gain is not None else None
    tp = m.ps(f"{tag}_tp", [P, NT, D])
    own = m.sem(f"{tag}_vector_chain")
    var_ready = m.sem(f"{tag}_var_ready")
    std_ready = m.sem(f"{tag}_std_ready")
    tile_ready = m.sem(f"{tag}_tile_ready")
    transposed = m.sem(f"{tag}_transposed")
    with nc.Block() as block:
        @block.vector
        def _(dve):
            chain = Chain(dve, own)
            for i in range(NT):
                last = nc.vector.bn_stats(stats[:, i, :], src[:, i, :])
            chain.link(last)
            for i in range(NT):
                last = nc.vector.bn_aggr(mv[:, i, :], stats[:, i, :])
            chain.link(last)
            if gain is None:
                nc.vector.tensor_scalar(var[:], mv[:, :, 1], eps, None, ALU.add).then_inc(var_ready, 1)
            else:
                chain.link(nc.vector.tensor_tensor(ms[:], mv[:, :, 0], mv[:, :, 0], ALU.mult))
                nc.vector.scalar_tensor_tensor(out=var[:], in0=ms[:], scalar=eps, in1=mv[:, :, 1],
                                               op0=ALU.add, op1=ALU.add).then_inc(var_ready, 1)
            dve.wait_ge(std_ready, 1)
            chain.link(nc.vector.reciprocal(rstd[:], std[:]))
            if gain is not None:
                for i in range(NT):
                    last = nc.vector.tensor_scalar(scaled[:, i, :], src[:, i, :], rstd[:, i:i + 1], None, ALU.mult)
                chain.link(last)
            for i in range(NT):
                if gain is None:
                    ins = nc.vector.tensor_scalar(out_tok[:, i, :], src[:, i, :], mv[:, i, 0:1], rstd[:, i:i + 1],
                                                  ALU.subtract, ALU.mult)
                else:
                    ins = nc.vector.tensor_tensor(out_tok[:, i, :], scaled[:, i, :], gain, ALU.mult)
                ins.then_inc(tile_ready, 1)

        @block.tensor
        def _(pe):
            for i in range(NT):
                pe.wait_ge(tile_ready, i + 1)
                nc.tensor.transpose(tp[:, i, :], out_tok[:, i, :], ident[:]).then_inc(transposed, 1)

        @block.scalar
        def _(act):
            act.wait_ge(var_ready, 1)
            nc.scalar.activation(std[:], var[:], ACT.Sqrt).then_inc(std_ready, 1)
            for b in range(2):
                act.wait_ge(transposed, 4 * b + 4)
                nc.scalar.activation(out_T[:, b * HALF:(b + 1) * HALF], tp[:, 4 * b:4 * b + 4, :], ACT.Copy)
    m.close()


def load_block(nc, A, T):
    m = Mem(nc)
    m8 = m.sb("m8", [P, 2, KT], U8)
    mf = m.sb("mf", [P, 2, KT])
    lane_any = m.sb("lane_any", [P, 2])
    pen = m.sb("pen", [P, 2, KT])
    penT = m.sb("penT", [KT, 2, P])
    penT16 = m.sb("penT16", [KT, 2, P], BF16)
    tp = m.ps("pen_tp", [KT, 4, P])[:, 0:2, :]
    zeroed = m.sem("mask_zeroed")
    loaded = m.sem("mask_loaded")
    small = m.sem("small_loaded")
    own = m.sem("load_vector_chain")
    lanes = m.sem("lane_any_ready")
    anyed = m.sem("any_ready")
    pens = m.sem("pen_ready")
    pent = m.sem("pen_transposed")
    copied = m.sem("penT_ready")
    stored = m.sem("pen_stored")
    with nc.Block() as block:
        @block.sync
        def _(sp):
            sp.wait_ge(zeroed, 1)
            for l in range(2):
                sp.dma_start(m8[:, l, 0:KF], A["masks"][l][0, 0:KF * P].rearrange("(p t) -> p t", t=KF)).then_inc(loaded, 16)
                sp.dma_start(m8[0:TAIL, l, KF:KT], A["masks"][l][0, KF * P:CTX].rearrange("(p t) -> p t", t=1)).then_inc(loaded, 16)
            sp.dma_start(T["x"][:], A["x"][0].rearrange("(i p) d -> p i d", p=P)).then_inc(small, 16)
            sp.dma_start(T["ident"][:], A["ident"]).then_inc(small, 16)
            sp.dma_start(T["g"][:, 0:2], A["g_xattn"].partition_broadcast(P)).then_inc(small, 16)
            sp.dma_start(T["g"][:, 2:4], A["g_ffn"].partition_broadcast(P)).then_inc(small, 16)
            sp.dma_start(T["ident16"][:], A["ident16"]).then_inc(small, 16)
            sp.wait_ge(copied, 2)
            sp.dma_start(T["pen16_dram"].rearrange("l (t p) -> t l p", p=P), penT16[:]).then_inc(stored, 16)
            sp.dma_start(T["rows32_dram"][1, :].rearrange("(t p) -> t p", p=P), penT[:, 1, :]).then_inc(stored, 16)
            sp.dma_start(T["rows32_dram"][0:1, :], A["ones32"][0:1, 0:KT * P]).then_inc(stored, 16)
            sp.wait_ge(stored, 48)
            sp.wait_ge(small, 80)

        @block.vector
        def _(dve):
            chain = Chain(dve, own)
            nc.vector.memset(m8[:], 0).then_inc(zeroed, 1)
            dve.wait_ge(loaded, 64)
            chain.link(nc.vector.tensor_copy(mf[:], m8[:]))
            nc.vector.tensor_reduce(lane_any[:], mf[:], AX.X, ALU.max).then_inc(lanes, 1)
            dve.wait_ge(anyed, 1)
            for l in range(2):
                ins = nc.vector.tensor_scalar(pen[:, l, :], mf[:, l, :], T["any"][:, l:l + 1], BIG,
                                              ALU.subtract, ALU.mult)
                ins.then_inc(pens, 1)
            dve.wait_ge(pent, 2)
            nc.vector.tensor_copy(penT16[:], tp[:]).then_inc(copied, 1)
            nc.vector.tensor_copy(penT[:], tp[:]).then_inc(copied, 1)

        @block.gpsimd
        def _(pool):
            pool.wait_ge(lanes, 1)
            nc.gpsimd.partition_all_reduce(T["any"][:], lane_any[:], P, RMAX).then_inc(anyed, 1)

        @block.tensor
        def _(pe):
            pe.wait_ge(small, 80)
            for l in range(2):
                pe.wait_ge(pens, l + 1)
                nc.tensor.transpose(tp[:, l, :], pen[:, l, :], T["ident"][:]).then_inc(pent, 1)

        @block.scalar
        def _(act):
            act.wait_ge(small, 80)
            nc.scalar.activation(T["tg"][:], T["g"][:], ACT.Tanh)
    m.close()


def context0_block(nc, A, T):
    m = Mem(nc)
    ctx_sb = m.sb("ctx_sb", [P, KT, CD])
    wk = m.sb("wk0", [CD, D])
    wv = m.sb("wv0", [CD, D])
    ctxT = m.sb("ctxT0", [CD, 2, CH])
    parts = m.sb("k0_parts", [P, 2, 3, CH], BF16)
    rest = m.sb("k0_rest", [P, 2, CH])
    tp = m.ps("ctx_tp", [CD, 2, CH])
    kp = m.ps("k0_ps", [P, 2, CH])
    vp = m.ps("v0_ps", [P, 2, 4, D])
    loaded = m.sem("ctx_loaded")
    wloaded = m.sem("w_loaded")
    transposed = m.sem("ctx_transposed")
    ctxT_ready = m.sem("ctxT_ready")
    keys = m.sem("keys_ready")
    vals = m.sem("values_ready")
    high = m.sem("high_ready")
    rest1 = m.sem("rest_ready")
    mid = m.sem("mid_ready")
    low = m.sem("low_ready")
    vcopied = m.sem("values_copied")
    stored = [m.sem(f"parts_stored{i}") for i in range(2)]
    V = T["V0"]
    with nc.Block() as block:
        @block.sync
        def _(sp):
            sp.dma_start(ctx_sb[:, 0:KF, :], A["ctx"][0, 0:KF * P, :].rearrange("(p t) d -> p t d", t=KF)).then_inc(loaded, 16)
            sp.dma_start(ctx_sb[0:TAIL, KF, :], A["ctx"][0, KF * P:CTX, :]).then_inc(loaded, 16)
            sp.dma_start(wk[:], A["L0_xattn_Wk"]).then_inc(wloaded, 16)
            sp.dma_start(wv[:], A["L0_xattn_Wv"]).then_inc(wloaded, 16)
            for c, (k0, n) in enumerate(CHUNKS):
                sp.wait_ge(low, c + 1)
                sp.wait_ge(mid, c + 1)
                sp.dma_start(T["k0_dram"][:, :, k0:k0 + n].rearrange("s c k -> c s k"),
                             parts[:, c % 2, :, 0:n]).then_inc(stored[c % 2], 16)
            for i in range(2):
                sp.wait_ge(stored[i], 16 * ((NC + 1 - i) // 2))

        @block.tensor
        def _(pe):
            pe.wait_ge(loaded, 32)

            def transposes(c):
                if c >= 2:
                    pe.wait_ge(ctxT_ready, c - 1)
                for t, n in tiles_of(c):
                    o = (t - 4 * c) * P
                    last = nc.tensor.transpose(tp[:, c % 2, o:o + n], ctx_sb[0:n, t, :], T["ident"][0:n, 0:n])
                last.then_inc(transposed, 1)

            transposes(0)
            for c, (k0, w) in enumerate(CHUNKS):
                if c + 1 < NC:
                    transposes(c + 1)
                if c == 0:
                    pe.wait_ge(wloaded, 32)
                pe.wait_ge(ctxT_ready, c + 1)
                if c >= 2:
                    pe.wait_ge(rest1, c - 1)
                    pe.wait_ge(vcopied, c - 1)
                nc.tensor.matmul(kp[:, c % 2, 0:w], wk[:], ctxT[:, c % 2, 0:w], start=True, stop=True).then_inc(keys, 1)
                for t, n in tiles_of(c):
                    o = (t - 4 * c) * P
                    last = nc.tensor.matmul(vp[0:n, c % 2, t - 4 * c, :], ctxT[:, c % 2, o:o + n], wv[:],
                                            start=True, stop=True)
                last.then_inc(vals, 1)

        @block.scalar
        def _(act):
            for c, (k0, w) in enumerate(CHUNKS):
                act.wait_ge(transposed, c + 1)
                if c >= 2:
                    act.wait_ge(vals, c - 1)
                nc.scalar.activation(ctxT[:, c % 2, 0:w], tp[:, c % 2, 0:w], ACT.Copy).then_inc(ctxT_ready, 1)
                act.wait_ge(keys, c + 1)
                if c >= 2:
                    act.wait_ge(stored[c % 2], 16 * (c // 2))
                nc.scalar.activation(parts[:, c % 2, 0, 0:w], kp[:, c % 2, 0:w], ACT.Copy).then_inc(high, 1)
                act.wait_ge(rest1, c + 1)
                nc.scalar.activation(parts[:, c % 2, 1, 0:w], rest[:, c % 2, 0:w], ACT.Copy).then_inc(mid, 1)

        @block.vector
        def _(dve):
            for c, (k0, w) in enumerate(CHUNKS):
                dve.wait_ge(high, c + 1)
                if c >= 2:
                    dve.wait_ge(low, c - 1)
                nc.vector.tensor_tensor(rest[:, c % 2, 0:w], kp[:, c % 2, 0:w], parts[:, c % 2, 0, 0:w],
                                        ALU.subtract).then_inc(rest1, 1)
                dve.wait_ge(vals, c + 1)
                full = [t for t, n in tiles_of(c) if n == P]
                ins = nc.vector.tensor_copy(V[:, 4 * c:4 * c + len(full), :, :].rearrange("p t h d -> p t (h d)"),
                                            vp[:, c % 2, 0:len(full), :])
                if c == NC - 1:
                    ins = nc.vector.tensor_copy(V[0:TAIL, KF, :, :].rearrange("p h d -> p (h d)"),
                                                vp[0:TAIL, c % 2, KF - 4 * c, :])
                ins.then_inc(vcopied, 1)
                dve.wait_ge(mid, c + 1)
                nc.vector.tensor_tensor(parts[:, c % 2, 2, 0:w], rest[:, c % 2, 0:w], parts[:, c % 2, 1, 0:w],
                                        ALU.subtract).then_inc(low, 1)
    m.close()


def operand_block(nc, tag, A, T, wq, qT_src, kT_src, q_any):
    m = Mem(nc)
    parts = m.sb(f"{tag}_parts", [P, 2, 3, HALF], BF16)
    rest = m.sb(f"{tag}_rest", [P, 2, HALF])
    val = m.sb(f"{tag}_val", [P, 2, HALF])
    qp = m.ps(f"{tag}_ps", [P, 2, HALF])
    projected = m.sem(f"{tag}_projected")
    vals = m.sem(f"{tag}_values")
    high = m.sem(f"{tag}_high")
    rest1 = m.sem(f"{tag}_rest1")
    mid = m.sem(f"{tag}_mid")
    low = m.sem(f"{tag}_low")
    wl = m.sem(f"{tag}_wl")
    stored = [m.sem(f"{tag}_stored{i}") for i in range(2)]
    zeroed = m.sem(f"{tag}_zeroed")
    gathered = m.sem(f"{tag}_gathered")
    srcs = [(qT_src, T["q_dram"])] + ([(kT_src, T["ks_dram"])] if kT_src is not None else [])
    jobs = [(s, hf) for s in range(len(srcs)) for hf in range(2)]
    W = m.sb(f"{tag}_w", [D, D]) if wq is not None else None
    Q2, K2 = T["Q2"], T["K2"]

    def queries(eng, s):
        for i in range(2):
            eng.wait_ge(stored[i], 16 * (len(jobs) // 2))
        eng.wait_ge(zeroed, 2)
        for j, (qpart, _) in enumerate(SPLIT):
            r = 2 + 16 * j + 8 * s
            for b in range(2):
                for hf in range(2):
                    src = T["q_dram"][qpart, :, hf * HALF:(hf + 1) * HALF].rearrange(
                        "(g b s d) q -> b s d g q", b=2, s=2, d=HD0)[b, s]
                    dst = Q2[r:r + HD0, :, :].rearrange("r (g f) (b s q) -> r f b s g q", f=2, b=2, s=2)[:, hf, b, s]
                    eng.dma_start(dst, src).then_inc(gathered, 16)

    def keys(eng):
        src = T["ks_dram"] if kT_src is not None else T["k0_dram"]
        for j, (_, kpart) in enumerate(SPLIT):
            eng.dma_start(K2[2 + 16 * j:18 + 16 * j, :, :],
                          src[kpart, :, :].rearrange("(pr c) k -> c pr k", c=16)).then_inc(gathered, 16)

    with nc.Block() as block:
        @block.sync
        def _(sp):
            if wq is not None:
                sp.dma_start(W[:], wq).then_inc(wl, 16)
            for i, (s, hf) in enumerate(jobs):
                sp.wait_ge(low, i + 1)
                sp.wait_ge(mid, i + 1)
                sp.dma_start(srcs[s][1][:, :, hf * HALF:(hf + 1) * HALF].rearrange("s c k -> c s k"),
                             parts[:, i % 2, :, :]).then_inc(stored[i % 2], 16)
            queries(sp, 0)
            if kT_src is not None:
                keys(sp)
            sp.dma_start(Q2[1:2, :, :], A["ones16"][0:1, 0:2 * N].unsqueeze(1).broadcast_to([1, NU0, 2 * N])).then_inc(gathered, 16)
            nk = CTX if kT_src is None else N
            sp.dma_start(K2[0:1, :, :], A["ones16"][0:1, 0:nk].unsqueeze(1).broadcast_to([1, H0 // 2, nk])).then_inc(gathered, 16)
            n = len(SPLIT) * 9 + 2
            if kT_src is None:
                sp.dma_start(K2[1:2, :, :], T["pen16_dram"][0:1, 0:CTX].unsqueeze(1).broadcast_to([1, H0 // 2, CTX])).then_inc(gathered, 16)
                n += 1
            sp.wait_ge(gathered, 16 * n)

        @block.tensor
        def _(pe):
            if wq is not None:
                pe.wait_ge(wl, 16)
                for hf in range(2):
                    nc.tensor.matmul(qp[:, hf, :], W[:], qT_src[:, hf * HALF:(hf + 1) * HALF],
                                     start=True, stop=True).then_inc(projected, 1)

        @block.scalar
        def _(act):
            if kT_src is None:
                keys(act)
            for i, (s, hf) in enumerate(jobs):
                src = srcs[s][0][:, hf * HALF:(hf + 1) * HALF]
                if i >= 2:
                    act.wait_ge(low, i - 1)
                if wq is not None:
                    act.wait_ge(projected, i + 1)
                    src = qp[:, hf, :]
                nc.scalar.activation(val[:, i % 2, :], src, ACT.Copy, scale=q_any if q_any is not None else 1.0).then_inc(vals, 1)
                act.wait_ge(vals, i + 1)
                if i >= 2:
                    act.wait_ge(stored[i % 2], 16 * (i // 2))
                nc.scalar.activation(parts[:, i % 2, 0, :], val[:, i % 2, :], ACT.Copy).then_inc(high, 1)
                act.wait_ge(rest1, i + 1)
                nc.scalar.activation(parts[:, i % 2, 1, :], rest[:, i % 2, :], ACT.Copy).then_inc(mid, 1)
            queries(act, 1)

        @block.vector
        def _(dve):
            for i in range(len(jobs)):
                dve.wait_ge(high, i + 1)
                if i >= 2:
                    dve.wait_ge(low, i - 1)
                nc.vector.tensor_tensor(rest[:, i % 2, :], val[:, i % 2, :], parts[:, i % 2, 0, :], ALU.subtract).then_inc(rest1, 1)
                dve.wait_ge(mid, i + 1)
                nc.vector.tensor_tensor(parts[:, i % 2, 2, :], rest[:, i % 2, :], parts[:, i % 2, 1, :], ALU.subtract).then_inc(low, 1)

        @block.gpsimd
        def _(pool):
            nc.gpsimd.memset(Q2[:].bitcast(U32), 0).then_inc(zeroed, 1)
            if kT_src is not None:
                nc.gpsimd.memset(K2[:].bitcast(U32), 0).then_inc(zeroed, 1)
            else:
                nc.gpsimd.memset(T["Vs"][:], 1.0).then_inc(zeroed, 1)
    m.close()


def attention0_block(nc, A, T):
    m = Mem(nc)
    K2, Q2, V, Vs, Oraw = T["K2"], T["Q2"], T["V0"], T["Vs"], T["Oraw"]
    NM = 16 * NC
    PAIRS = 2 * KT
    SHIFT_PAIR = PAIRS - 7
    scale = float(HD0) ** -0.5
    probs = m.sb("probs0", [P, PROB_RING0, 2 * HALF])
    cmax = m.sb("cmax0", [P, NM])
    negm = m.sb("negm0", [P, 16])
    negmT = m.sb("negmT0", [16, P], BF16)
    zeros = m.sb("zeros0", [P, HALF])
    sp2 = m.ps("scores0", [P, SCORE_RING, 2, HALF])
    mp = m.ps("maxps0", [P, MAX_RING0, HALF])
    acc = m.ps("acc0", [P, HALF])
    scored = m.sem("a0_scored")
    probs_ready = m.sem("a0_probs_ready")
    weighed = m.sem("a0_weighed")
    acc_free = m.sem("a0_acc_free")
    mscored = m.sem("a0_max_scored")
    maxed = m.sem("a0_maxed")
    negm_ready = m.sem("a0_negm_ready")
    shift_ready = m.sem("a0_shift_ready")
    shift_stored = m.sem("a0_shift_stored")
    negmT_ready = m.sem("a0_negmT_ready")
    vs_ready = m.sem("a0_vs_ready")
    zer = m.sem("a0_zeros")
    tail_reached = m.sem("a0_tail_reached")
    shift_loading = m.sem("a0_shift_loading")

    def key_tile(t):
        return P if t < KF else TAIL


    with nc.Block() as block:
        @block.tensor
        def _(pe):
            def max_matmul(u, n):
                q, c = divmod(n, NC)
                j = q // 4
                k0, w = CHUNKS[c]
                bank = n % MAX_RING0
                back = back_in_ring(n, NM + 1, MAX_RING0)
                pe.wait_ge(maxed, (NM + 1) * u + n - back + 1 + MAX_CREDIT)
                nc.tensor.matmul(mp[:, bank, 0:w],
                                 Q2[0:ROWS, ds(u, 1), q * P:(q + 1) * P].rearrange("r a q -> r (a q)"),
                                 K2[0:ROWS, ds(u // 2 * 2 + j // 2, 1), k0:k0 + w].rearrange("r a k -> r (a k)"),
                                 start=True, stop=True).then_inc(mscored, 1)

            def shift_transpose(u):
                bank = NM % MAX_RING0
                pe.wait_ge(negm_ready, u + 1)
                nc.tensor.transpose(mp[0:16, bank, 0:P], negm[:], T["ident"][:]).then_inc(mscored, 1)

            def score(u, t, b):
                n = PAIRS * u + 2 * t + b
                kn = key_tile(t)
                pe.wait_ge(probs_ready, n + 1)
                if t == KT - 1:
                    pe.sem_inc(tail_reached, 1)
                for i in range(2):
                    j = 2 * b + i
                    ins = nc.tensor.matmul(sp2[0:kn, b, i, :],
                                           K2[0:ROWS, ds(u // 2 * 2 + b, 1), t * P:t * P + kn].rearrange("r a k -> r (a k)"),
                                           Q2[0:ROWS, ds(u, 1), j * HALF:(j + 1) * HALF].rearrange("r a q -> r (a q)"),
                                           start=True, stop=True)
                ins.then_inc(scored, 1)

            def weigh(u, t):
                kn = key_tile(t)
                pe.wait_ge(probs_ready, PAIRS * u + 2 * t + 2 + SCORE_RING)
                if t == KT - 1:
                    pe.sem_inc(tail_reached, 1)
                for j in range(GH):
                    ins = nc.tensor.matmul(acc[32 * j:32 * j + VW, :], Vs[0:kn, t, j, :],
                                           probs[0:kn, (2 * t + j // 2) % PROB_RING0, (j % 2) * HALF:(j % 2 + 1) * HALF],
                                           start=(t == 0), stop=(t == KT - 1), skip_group_check=True)
                ins.then_inc(weighed, 2)

            def unit(u, nxt):
                pe.wait_ge(shift_ready, 16 * u + 16)
                done = 0
                for t in range(KT):
                    for b in range(2):
                        i = 2 * t + b
                        score(u, t, b)
                        if nxt is not None:
                            want = min(NM, (i + 1) * NM // (SHIFT_PAIR - 2) + 1)
                            while done < want:
                                max_matmul(nxt, done)
                                done += 1
                            if i == SHIFT_PAIR:
                                shift_transpose(nxt)
                    if t >= 1:
                        if t == 1:
                            pe.wait_ge(acc_free, u + 1)
                            pe.wait_ge(vs_ready, 3 * u + 1)
                        if t - 1 == MID_TILE:
                            pe.wait_ge(vs_ready, 3 * u + 3)
                        weigh(u, t - 1)
                weigh(u, KT - 1)

            pe.sem_inc(weighed, PROB_RING0)
            pe.wait_ge(zer, 1)
            nc.tensor.matmul(acc[:], zeros[:, 0:P], zeros[:], start=True, stop=True)
            for n in range(NM):
                max_matmul(0, n)
            shift_transpose(0)
            with pe.Fori(0, NU0 - 1) as u:
                unit(u, u + 1)
            unit(NU0 - 1, None)

        @block.vector
        def _(dve):
            def maxima(u, first):
                for n in range(NM):
                    w = CHUNKS[n % NC][1]
                    dve.wait_ge(mscored, (NM + 1) * u + n + 1)
                    nc.vector.tensor_reduce(cmax[:, n:n + 1], mp[:, n % MAX_RING0, 0:w], AX.X,
                                            ALU.max).then_inc(maxed, 1)
                dve.wait_ge(maxed, (NM + 1) * u + NM + MAX_CREDIT)
                nc.vector.tensor_reduce(negm[:], cmax[:].rearrange("p (q c) -> p q c", c=NC), AX.X, ALU.max,
                                        negate=True).then_inc(negm_ready, 1)
                dve.wait_ge(mscored, (NM + 1) * u + NM + 1)
                if not first:
                    dve.wait_ge(shift_ready, 16 * u)
                nc.vector.tensor_copy(negmT[:], mp[0:16, NM % MAX_RING0, 0:P]).then_inc(negmT_ready, 1)
                dve.wait_ge(negmT_ready, u + 1)
                dve.sem_inc(maxed, 1)

            nc.vector.memset(zeros[:], 0.0).then_inc(zer, 1)
            dve.sem_inc(maxed, MAX_CREDIT)
            maxima(0, True)
            with dve.Fori(1, NU0) as u:
                maxima(u, False)

        @block.scalar
        def _(act):
            act.sem_inc(probs_ready, SCORE_RING)
            act.sem_inc(acc_free, 1)
            with act.Fori(0, NU0) as u:
                for t in range(KT):
                    kn = key_tile(t)
                    for b in range(2):
                        n = PAIRS * u + 2 * t + b
                        act.wait_ge(scored, n + 1)
                        act.wait_ge(weighed, n + 1)
                        nc.scalar.activation(probs[0:kn, (2 * t + b) % PROB_RING0, :],
                                             sp2[0:kn, b, :, :].rearrange("p i q -> p (i q)"), ACT.Exp,
                                             scale=scale).then_inc(probs_ready, 1)
                act.wait_ge(weighed, PAIRS * u + PAIRS + PROB_RING0)
                nc.scalar.activation(Oraw[:, ds(u, 1), :].rearrange("p a q -> p (a q)"), acc[:], ACT.Copy).then_inc(acc_free, 1)

        @block.gpsimd
        def _(pool):
            def stage(u, part):
                t0, t1 = ((0, MID_TILE), (MID_TILE, KF))[part]
                g = u // 2
                nc.gpsimd.tensor_copy(
                    Vs[:, t0:t1, :, 0:HD0],
                    V[:, t0:t1, ds(g * GH, GH), :]).then_inc(vs_ready, 1)
                if part:
                    nc.gpsimd.tensor_copy(Vs[0:TAIL, KF, :, 0:HD0], V[0:TAIL, KF, ds(g * GH, GH), :]).then_inc(vs_ready, 1)

            stage(0, 0)
            stage(0, 1)
            with pool.Fori(1, NU0) as u:
                pool.wait_ge(weighed, PAIRS * u - PAIRS + 2 * MID_TILE + PROB_RING0)
                stage(u, 0)
                pool.wait_ge(weighed, PAIRS * u + PROB_RING0)
                stage(u, 1)

        @block.sync
        def _(sp):
            with sp.Fori(0, NU0) as u:
                sp.wait_ge(negmT_ready, u + 1)
                sp.dma_start(T["shift0_dram"][ds(u, 1), :].rearrange("a (j p) -> (a j) p", p=P), negmT[:]).then_inc(shift_stored, 16)
                sp.wait_ge(shift_stored, 16 * u + 16)
                sp.sem_inc(shift_loading, 1)
                sp.dma_start(Q2[0:1, ds(u, 1), :], T["shift0_dram"][ds(u, 1), :].unsqueeze(0)).then_inc(shift_ready, 16)
    m.close()


def project_block(nc, tag, A, T, Oraw, wo, out, base, factor):
    m = Mem(nc)
    pick = m.sb(f"{tag}_pick", [P, NU0, 32])
    spreader = m.sb(f"{tag}_spreader", [P, NU0, P])
    inv = m.sb(f"{tag}_inv", [P, HALF])
    wox = m.sb(f"{tag}_wox", [P, NG, D])
    on = Oraw
    sums = m.ps(f"{tag}_sums", [P, HALF])
    rp = m.ps(f"{tag}_rp", [P, 2, HALF])
    yp = m.ps(f"{tag}_yp", [P, 2, 4, D])
    loaded = m.sem(f"{tag}_loaded")
    zeroed = m.sem(f"{tag}_zeroed")
    spread = m.sem(f"{tag}_spread")
    picked = m.sem(f"{tag}_picked")
    recip = m.sem(f"{tag}_recip")
    normed = m.sem(f"{tag}_normed")
    projected = m.sem(f"{tag}_projected")
    with nc.Block() as block:
        @block.sync
        def _(sp):
            sp.dma_start(pick[:], A["sumpick"]).then_inc(loaded, 16)
            sp.dma_start(spreader[:], A["sumspread"]).then_inc(loaded, 16)
            sp.wait_ge(zeroed, 1)
            for j in range(GH):
                sp.dma_start(wox[32 * j:32 * j + HD0, :, :],
                             wo.rearrange("(g j d) n -> j d g n", j=GH, d=HD0)[j]).then_inc(loaded, 16)

        @block.gpsimd
        def _(pool):
            nc.gpsimd.memset(wox[:], 0.0).then_inc(zeroed, 1)

        @block.tensor
        def _(pe):
            pe.wait_ge(loaded, 16 * (2 + GH))
            for u in range(NU0):
                c = 32 * (u % 4)
                last = nc.tensor.matmul(sums[c:c + 32, :], pick[:, u, :], Oraw[:, u, :], start=(u < 4), stop=(u >= 4),
                                        skip_group_check=True)
            last.then_inc(picked, 1)
            pe.wait_ge(recip, 1)
            for u in range(NU0):
                if u >= 2:
                    pe.wait_ge(normed, u - 1)
                nc.tensor.matmul(rp[:, u % 2, :], spreader[:, u, :], inv[:], start=True, stop=True).then_inc(spread, 1)
            pe.wait_ge(normed, NU0)
            for f in range(2):
                for i in range(4):
                    for g in range(NG):
                        last = nc.tensor.matmul(yp[:, f, i, :], on[:, 2 * g + f, i * P:(i + 1) * P], wox[:, g, :],
                                                start=(g == 0), stop=(g == NG - 1))
                last.then_inc(projected, 1)

        @block.vector
        def _(dve):
            dve.wait_ge(picked, 1)
            nc.vector.reciprocal(inv[:], sums[:]).then_inc(recip, 1)
            for u in range(NU0):
                dve.wait_ge(spread, u + 1)
                nc.vector.tensor_tensor(on[:, u, :], Oraw[:, u, :], rp[:, u % 2, :], ALU.mult).then_inc(normed, 1)
            for f in range(2):
                dve.wait_ge(projected, f + 1)
                o, b, y = out[:, 4 * f:4 * f + 4, :], base[:, 4 * f:4 * f + 4, :], yp[:, f, :, :]
                if factor is None:
                    nc.vector.tensor_tensor(o, y, b, ALU.add)
                else:
                    nc.vector.scalar_tensor_tensor(out=o, in0=y, scalar=factor, in1=b, op0=ALU.mult, op1=ALU.add)
    m.close()


def gate_block(nc, tag, A, T, xT, gate_w, comb, cap):
    E = 8
    m = Mem(nc)
    gw = m.sb(f"{tag}_gw", [P, E])
    L = m.sb(f"{tag}_L", [P, NT, E])
    top = m.sb(f"{tag}_top", [P, NT, 8])
    idx = m.sb(f"{tag}_idx", [P, NT, 8], U32)
    idf = m.sb(f"{tag}_idf", [P, NT, 8])
    w = m.sb(f"{tag}_w", [P, NT, 2])
    one = m.sb(f"{tag}_one", [P, 2, NT, E])
    dif = m.sb(f"{tag}_dif", [P, NT])
    ex = m.sb(f"{tag}_ex", [P, NT])
    den = m.sb(f"{tag}_den", [P, NT])
    sh = m.sb(f"{tag}_sh", [P, NT, E])
    pr = m.sb(f"{tag}_pr", [P, NT, E])
    G = m.sb(f"{tag}_G", [P, NT, E])
    hot = m.sb(f"{tag}_hot", [P, NT, E])
    cand = m.sb(f"{tag}_cand", [P, NT, E])
    ranks = m.sb(f"{tag}_ranks", [E, 2, N])
    best = m.sb(f"{tag}_best", [E, 2, 8])
    kept = m.sb(f"{tag}_kept", [E, N])
    lp = m.ps(f"{tag}_lp", [P, NT, HALF // NT])[:, :, 0:E]
    cp = m.ps(f"{tag}_cp", [E, N])
    bp = m.ps(f"{tag}_bp", [P, NT, HALF // NT])[:, :, 0:E]
    loaded = m.sem(f"{tag}_loaded")
    logits = m.sem(f"{tag}_logits")
    own = m.sem(f"{tag}_vector_chain")
    dif_ready = m.sem(f"{tag}_dif_ready")
    ex_ready = m.sem(f"{tag}_ex_ready")
    cand_ready = m.sem(f"{tag}_cand_ready")
    candT = m.sem(f"{tag}_cand_transposed")
    kept_ready = m.sem(f"{tag}_kept_ready")
    keptT = m.sem(f"{tag}_kept_transposed")
    iota = T["iota8"]
    with nc.Block() as block:
        @block.sync
        def _(sp):
            sp.dma_start(gw[:], gate_w).then_inc(loaded, 16)
            sp.dma_start(iota[:], A["iota8"].partition_broadcast(P)).then_inc(loaded, 16)

        @block.tensor
        def _(pe):
            pe.wait_ge(loaded, 32)
            for i in range(NT):
                last = nc.tensor.matmul(lp[:, i, :], xT[:, i * P:(i + 1) * P], gw[:], start=True, stop=True)
            last.then_inc(logits, 1)
            if cap:
                pe.wait_ge(cand_ready, 1)
                for i in range(NT):
                    last = nc.tensor.transpose(cp[:, i * P:(i + 1) * P], cand[:, i, :], T["ident"][:])
                last.then_inc(candT, 1)
                pe.wait_ge(kept_ready, 1)
                for i in range(NT):
                    last = nc.tensor.transpose(bp[:, i, :], kept[:, i * P:(i + 1) * P], T["ident"][0:E, 0:E])
                last.then_inc(keptT, 1)

        @block.scalar
        def _(act):
            act.wait_ge(dif_ready, 1)
            if cap:
                nc.scalar.activation(pr[:], sh[:], ACT.Exp).then_inc(ex_ready, 1)
            else:
                nc.scalar.activation(ex[:], dif[:], ACT.Exp).then_inc(ex_ready, 1)

        @block.vector
        def _(dve):
            chain = Chain(dve, own)
            dve.wait_ge(logits, 1)
            dve.wait_ge(loaded, 32)
            chain.link(nc.vector.tensor_copy(L[:], lp[:]))
            score = L
            if cap:
                chain.link(nc.vector.tensor_reduce(dif[:], L[:], AX.X, ALU.max))
                nc.vector.tensor_tensor(sh[:], L[:], dif[:].unsqueeze(2).broadcast_to([P, NT, E]),
                                        ALU.subtract).then_inc(dif_ready, 1)
                dve.wait_ge(ex_ready, 1)
                chain.link(nc.vector.tensor_reduce(den[:], pr[:], AX.X, ALU.add))
                chain.link(nc.vector.reciprocal(ex[:], den[:]))
                chain.link(nc.vector.tensor_tensor(sh[:], pr[:], ex[:].unsqueeze(2).broadcast_to([P, NT, E]), ALU.mult))
                score = sh
            for i in range(NT):
                last = nc.vector.max(top[:, i, :], score[:, i, :])
            chain.link(last)
            for i in range(NT):
                last = nc.vector.max_index(idx[:, i, :], top[:, i, :], score[:, i, :])
            chain.link(last)
            chain.link(nc.vector.tensor_copy(idf[:], idx[:]))
            if cap:
                chain.link(nc.vector.tensor_copy(w[:], top[:, :, 0:2]))
            else:
                nc.vector.tensor_tensor(dif[:], top[:, :, 1], top[:, :, 0], ALU.subtract).then_inc(dif_ready, 1)
                dve.wait_ge(ex_ready, 1)
                chain.link(nc.vector.tensor_scalar(den[:], ex[:], 1.0, None, ALU.add))
                chain.link(nc.vector.reciprocal(w[:, :, 0], den[:]))
                chain.link(nc.vector.tensor_tensor(w[:, :, 1], ex[:], w[:, :, 0], ALU.mult))
            for i in range(NT):
                for s in range(2):
                    last = nc.vector.tensor_scalar(one[:, s, i, :], iota[:], idf[:, i, s:s + 1], w[:, i, s:s + 1],
                                                   ALU.is_equal, ALU.mult)
            chain.link(last)
            dst = G if cap else comb
            chain.link(nc.vector.tensor_tensor(dst[:], one[:, 0, :, :], one[:, 1, :, :], ALU.add))
            if cap:
                for i in range(NT):
                    for s in range(2):
                        last = nc.vector.tensor_scalar(one[:, s, i, :], iota[:], idf[:, i, s:s + 1], None, ALU.is_equal)
                chain.link(last)
                chain.link(nc.vector.tensor_tensor(hot[:], one[:, 0, :, :], one[:, 1, :, :], ALU.add))
                nc.vector.scalar_tensor_tensor(out=cand[:], in0=hot[:], scalar=-1.0, in1=G[:], op0=ALU.add,
                                               op1=ALU.add).then_inc(cand_ready, 1)
                dve.wait_ge(candT, 1)
                chain.link(nc.vector.tensor_copy(ranks[:, 0, :], cp[:]))
                for r in range(cap // 8):
                    chain.link(nc.vector.max(best[:, r % 2, :], ranks[:, r % 2, :]))
                    chain.link(nc.vector.match_replace(ranks[:, (r + 1) % 2, :], best[:, r % 2, :], ranks[:, r % 2, :], -2.0))
                nc.vector.tensor_scalar(kept[:], ranks[:, (cap // 8) % 2, :], -2.0, None, ALU.is_equal).then_inc(kept_ready, 1)
                dve.wait_ge(keptT, 1)
                nc.vector.tensor_tensor(comb[:], G[:], bp[:], ALU.mult)
    m.close()


def experts_block(nc, tag, A, T, xT, comb, w1, b1, w2, b2, F, func, out, base, factor, add):
    E = 8
    C = F // P
    m = Mem(nc)
    W1 = m.sb(f"{tag}_w1", [P, E, F])
    W2 = m.sb(f"{tag}_w2", [P, E, C, D])
    hT = m.sb(f"{tag}_hT", [P, 2, C, N])
    acc = m.sb(f"{tag}_acc", [P, NT, D])
    tot = m.sb(f"{tag}_tot", [P, NT, D])
    b1r = m.sb(f"{tag}_b1r", [E * C, P])
    b1T = m.sb(f"{tag}_b1T", [P, E * C])
    b2s = m.sb(f"{tag}_b2s", [E, D])
    combT = m.sb(f"{tag}_combT", [E, N])
    hp = m.ps(f"{tag}_hp", [P, 2, 2, HALF])
    yp = m.ps(f"{tag}_yp", [P, 2, 4, D])
    bp = m.ps(f"{tag}_bp", [P, 2, HALF])
    loaded = [m.sem(f"{tag}_w_loaded{e}") for e in range(E)]
    bl = m.sem(f"{tag}_b_loaded")
    upped = m.sem(f"{tag}_upped")
    acted = m.sem(f"{tag}_acted")
    downed = m.sem(f"{tag}_downed")
    added = m.sem(f"{tag}_added")
    b1t = m.sem(f"{tag}_b1t")
    b1c = m.sem(f"{tag}_b1c")
    cbt = m.sem(f"{tag}_cbt")
    cbc = m.sem(f"{tag}_cbc")
    biased = m.sem(f"{tag}_biased")
    own = m.sem(f"{tag}_vector_chain")
    with nc.Block() as block:
        @block.sync
        def _(sp):
            if b1 is not None:
                sp.dma_start(b1r[:], b1.rearrange("e (c p) -> (e c) p", p=P)).then_inc(bl, 16)
                sp.dma_start(b2s[:], b2).then_inc(bl, 16)
            for e in range(E):
                sp.dma_start(W1[:, e, :], w1[e]).then_inc(loaded[e], 16)
                sp.dma_start(W2[:, e, :, :], w2[e].rearrange("(c p) n -> p c n", p=P)).then_inc(loaded[e], 16)

        @block.tensor
        def _(pe):
            if b1 is not None:
                pe.wait_ge(bl, 32)
                nc.tensor.transpose(bp[:, 0, 0:E * C], b1r[:], T["ident"][0:E * C, 0:E * C]).then_inc(b1t, 1)

            def down(e):
                pe.wait_ge(acted, C * (e + 1))
                for b in range(2):
                    if e >= 1 or b1 is not None:
                        pe.wait_ge(added, 2 * (e - 1) + b + 1 + (2 if b1 is not None else 0))
                    for i in range(4 * b, 4 * b + 4):
                        for c in range(C):
                            last = nc.tensor.matmul(yp[:, b, i - 4 * b, :], hT[:, e % 2, c, i * P:(i + 1) * P],
                                                    W2[:, e, c, :], start=(c == 0), stop=(c == C - 1))
                    last.then_inc(downed, 1)

            for e in range(E):
                pe.wait_ge(loaded[e], 32)
                for c in range(C):
                    n = e * C + c
                    if n >= 2:
                        pe.wait_ge(acted, n - 1)
                    for hf in range(2):
                        last = nc.tensor.matmul(hp[:, n % 2, hf, :], W1[:, e, c * P:(c + 1) * P],
                                                xT[:, hf * HALF:(hf + 1) * HALF], start=True, stop=True)
                    last.then_inc(upped, 1)
                if e == 0 and b1 is not None:
                    pe.wait_ge(b1c, 1)
                    for i in range(NT):
                        last = nc.tensor.transpose(bp[0:E, i // 4, (i % 4) * P:(i % 4 + 1) * P], comb[:, i, :], T["ident"][:])
                    last.then_inc(cbt, 1)
                    pe.wait_ge(cbc, 1)
                    for i in range(NT):
                        last = nc.tensor.matmul(yp[:, i // 4, i % 4, :], combT[:, i * P:(i + 1) * P], b2s[:], start=True, stop=True)
                    last.then_inc(biased, 1)
                if e >= 1:
                    down(e - 1)
            down(E - 1)

        @block.scalar
        def _(act):
            if b1 is not None:
                act.wait_ge(b1t, 1)
                nc.scalar.activation(b1T[:], bp[:, 0, 0:E * C], ACT.Copy).then_inc(b1c, 1)
                act.wait_ge(b1c, 1)
            for e in range(E):
                for c in range(C):
                    n = e * C + c
                    act.wait_ge(upped, n + 1)
                    if e >= 2:
                        act.wait_ge(downed, 2 * (e - 1))
                    nc.scalar.activation(hT[:, e % 2, c, :], hp[:, n % 2, :, :].rearrange("p a q -> p (a q)"), func,
                                         bias=b1T[:, n:n + 1] if b1 is not None else 0.0).then_inc(acted, 1)

        @block.vector
        def _(dve):
            chain = Chain(dve, own)
            k = 0
            if b1 is not None:
                dve.wait_ge(cbt, 1)
                nc.vector.tensor_copy(combT[:], bp[0:E, :, :].rearrange("p a q -> p (a q)")).then_inc(cbc, 1)
                dve.wait_ge(biased, 1)
                for b in range(2):
                    nc.vector.tensor_copy(acc[:, 4 * b:4 * b + 4, :], yp[:, b, :, :]).then_inc(added, 1)
                    k += 1
            for e in range(E):
                for b in range(2):
                    dve.wait_ge(downed, 2 * e + b + 1)
                    if k >= 2:
                        dve.wait_ge(added, k - 1)
                    for i in range(4 * b, 4 * b + 4):
                        if k < 2:
                            last = nc.vector.tensor_scalar(acc[:, i, :], yp[:, b, i - 4 * b, :], comb[:, i, e:e + 1], None, ALU.mult)
                        else:
                            last = nc.vector.scalar_tensor_tensor(out=acc[:, i, :], in0=yp[:, b, i - 4 * b, :],
                                                                  scalar=comb[:, i, e:e + 1], in1=acc[:, i, :],
                                                                  op0=ALU.mult, op1=ALU.add)
                    last.then_inc(added, 1)
                    k += 1
            dve.wait_ge(added, k)
            src = acc
            if add is not None:
                chain.link(nc.vector.tensor_tensor(tot[:], acc[:], add[:], ALU.add))
                src = tot
            nc.vector.scalar_tensor_tensor(out=out[:], in0=src[:], scalar=factor, in1=base[:], op0=ALU.mult, op1=ALU.add)
    m.close()


def query1_block(nc, A, T):
    m = Mem(nc)
    wq = m.sb("wq1", [P, H1 * HD1])
    wk = m.sb("wk1", [CD, H1 * HD1])
    wT = m.sb("wT1", [P, 2, H1 // 2, P])
    M = m.sb("qk1", [P, 2, CD])
    val = m.sb("q1_val", [CD, 2, HALF])
    wp = m.ps("w1_tp", [P, 2, HALF])
    gp = m.ps("m1_ps", [P, 2, HALF])
    qp = m.ps("q1_ps", [CD, 2, HALF])
    wloaded = m.sem("c1_wloaded")
    rows = m.sem("c1_rows")
    zer = m.sem("c1_zeroed")
    wt = m.sem("c1_w_transposed")
    wtc = m.sem("c1_wT_copied")
    mready = m.sem("c1_m_ready")
    mcopied = m.sem("c1_m_copied")
    qready = m.sem("c1_q_ready")
    vals = m.sem("c1_q_values")
    high = m.sem("c1_q_high")
    low = m.sem("c1_q_low")
    rounded = m.sem("c1_q_rounded")
    qH, qL, q16 = T["qH"], T["qL"], T["q16"]
    jobs = [(w, c) for c in range(H1 // 2) for w in range(2)]
    with nc.Block() as block:
        @block.sync
        def _(sp):
            sp.dma_start(wq[:], A["L1_xattn_W_q"]).then_inc(wloaded, 16)
            sp.dma_start(wk[:], A["L1_xattn_W_k"]).then_inc(wloaded, 16)
            sp.dma_start(qH[CD + 1:CD + 2, :, :].bitcast(F32),
                         T["rows32_dram"][0:1, 0:N].unsqueeze(1).broadcast_to([1, H1, N])).then_inc(rows, 16)
            sp.wait_ge(zer, 1)
            sp.dma_start(q16[CD + 1:CD + 2, :, :], A["ones16"][0:1, 0:N].unsqueeze(1).broadcast_to([1, H1, N])).then_inc(rows, 16)
            sp.wait_ge(rows, 32)

        @block.gpsimd
        def _(pool):
            nc.gpsimd.memset(q16[CD:CR, :, :].bitcast(U32), 0).then_inc(zer, 1)

        @block.tensor
        def _(pe):
            pe.wait_ge(wloaded, 32)
            for n, (w, c) in enumerate(jobs):
                src = (wq, wk)[w]
                k = P if w == 0 else CD
                if n >= 2:
                    pe.wait_ge(wtc, n - 1)
                nc.tensor.transpose(wp[:, n % 2, 0:k], src[:, c * P:(c + 1) * P], T["ident"][0:k, 0:k]).then_inc(wt, 1)
            pe.wait_ge(wtc, len(jobs))

            def product(h):
                r = HD1 * (h % 2)
                if h >= 2:
                    pe.wait_ge(mcopied, h - 1)
                nc.tensor.matmul(gp[:, h % 2, 0:CD], wT[r:r + HD1, 0, h // 2, :], wT[r:r + HD1, 1, h // 2, 0:CD],
                                 start=True, stop=True).then_inc(mready, 1)

            product(0)
            for h in range(H1):
                if h + 1 < H1:
                    product(h + 1)
                pe.wait_ge(mcopied, h + 1)
                for hf in range(2):
                    n = 2 * h + hf
                    if n >= 2:
                        pe.wait_ge(vals, n - 1)
                    nc.tensor.matmul(qp[:, hf, :], M[:, h % 2, :], T["xT"][:, hf * HALF:(hf + 1) * HALF],
                                     start=True, stop=True).then_inc(qready, 1)

        @block.scalar
        def _(act):
            for n in range(2 * H1):
                h, hf = divmod(n, 2)
                act.wait_ge(qready, n + 1)
                if n >= 2:
                    act.wait_ge(low, n - 1)
                    act.wait_ge(rounded, n - 1)
                nc.scalar.activation(val[:, hf, :], qp[:, hf, :], ACT.Copy, scale=T["any"][0:CD, 1:2]).then_inc(vals, 1)
                act.wait_ge(vals, n + 1)
                nc.scalar.activation(q16[0:CD, h, hf * HALF:(hf + 1) * HALF], val[:, hf, :], ACT.Copy).then_inc(rounded, 1)

        @block.vector
        def _(dve):
            for n, (w, c) in enumerate(jobs):
                dve.wait_ge(wt, n + 1)
                k = P if w == 0 else CD
                nc.vector.tensor_copy(wT[:, w, c, 0:k], wp[:, n % 2, 0:k]).then_inc(wtc, 1)

            def copy_m(h):
                dve.wait_ge(mready, h + 1)
                if h >= 2:
                    dve.wait_ge(qready, 2 * (h - 1))
                nc.vector.tensor_copy(M[:, h % 2, :], gp[:, h % 2, 0:CD]).then_inc(mcopied, 1)

            copy_m(0)
            for n in range(2 * H1):
                h, hf = divmod(n, 2)
                if hf == 0 and h + 1 < H1:
                    copy_m(h + 1)
                q = slice(hf * HALF, (hf + 1) * HALF)
                dve.wait_ge(vals, n + 1)
                nc.vector.tensor_copy(qH[0:CD, h, q], val[:, hf, :]).then_inc(high, 1)
                dve.wait_ge(high, n + 1)
                nc.vector.tensor_tensor(qL[:, h, q], val[:, hf, :], qH[0:CD, h, q].bitcast(F32), ALU.subtract).then_inc(low, 1)
    m.close()


def context1_block(nc, A, T):
    m = Mem(nc)
    ctx_sb = m.sb("ctx1_sb", [P, KT, CD])
    wv = m.sb("wv1", [CD, H1 * HD1])
    ctxT = m.sb("ctxT1", [CD, 2, CH])
    vb = m.sb("vb1", [P, 2, H1, 4 * HD1])
    tp = m.ps("ctx1_tp", [CD, 2, CH])
    vp = m.ps("v1_ps", [P, 4, HALF])
    loaded = m.sem("c1_loaded")
    wloaded = m.sem("c1_wv_loaded")
    rows = m.sem("c1_key_rows")
    zer = m.sem("c1_vb_zeroed")
    transposed = m.sem("c1_transposed")
    ctxT_ready = m.sem("c1_ctxT_ready")
    high = m.sem("c1_high")
    low = m.sem("c1_low")
    valued = m.sem("c1_valued")
    vcopied = m.sem("c1_vcopied")
    stored = [m.sem(f"c1_stored{i}") for i in range(2)]
    cH, cL, cT16 = T["cH"], T["cL"], T["cT16"]
    with nc.Block() as block:
        @block.sync
        def _(sp):
            sp.dma_start(ctx_sb[:, 0:KF, :], A["ctx"][0, 0:KF * P, :].rearrange("(p t) d -> p t d", t=KF)).then_inc(loaded, 16)
            sp.dma_start(ctx_sb[0:TAIL, KF, :], A["ctx"][0, KF * P:CTX, :]).then_inc(loaded, 16)
            sp.dma_start(wv[:], A["L1_xattn_W_v"]).then_inc(wloaded, 16)
            sp.dma_start(cH[CD:CR, :].bitcast(F32), T["rows32_dram"]).then_inc(rows, 16)
            sp.dma_start(cT16[CD:CD + 1, :], A["ones16"][0:1, 0:CTX]).then_inc(rows, 16)
            sp.dma_start(cT16[CD + 1:CR, :], T["pen16_dram"][1:2, 0:CTX]).then_inc(rows, 16)
            for c in range(NC):
                nt = len(tiles_of(c))
                sp.wait_ge(vcopied, min(4 * c + 4, KT))
                sp.dma_start(T["v1_dram"][:, :, 4 * c:4 * c + nt, :].rearrange("h p t d -> p h (t d)"),
                             vb[:, c % 2, :, 0:nt * HD1]).then_inc(stored[c % 2], 16)
            for i in range(2):
                sp.wait_ge(stored[i], 16 * ((NC + 1 - i) // 2))
            sp.wait_ge(rows, 48)

        @block.gpsimd
        def _(pool):
            nc.gpsimd.memset(vb[:], 0.0).then_inc(zer, 1)
            nc.gpsimd.memset(cH[0:CD, CTX:KT * P].bitcast(F32), 0.0)
            nc.gpsimd.memset(cL[:, CTX:KT * P].bitcast(F32), 0.0)

        @block.tensor
        def _(pe):
            def transposes(c):
                if c >= 2:
                    pe.wait_ge(ctxT_ready, c - 1)
                for t, n in tiles_of(c):
                    o = (t - 4 * c) * P
                    last = nc.tensor.transpose(tp[:, c % 2, o:o + n], ctx_sb[0:n, t, :], T["ident"][0:n, 0:n])
                last.then_inc(transposed, 1)

            pe.wait_ge(loaded, 32)
            transposes(0)
            pe.wait_ge(wloaded, 16)
            for c in range(NC):
                if c + 1 < NC:
                    transposes(c + 1)
                pe.wait_ge(ctxT_ready, c + 1)
                for t, n in tiles_of(c):
                    o = (t - 4 * c) * P
                    if t >= 4:
                        pe.wait_ge(vcopied, t - 3)
                    nc.tensor.matmul(vp[0:n, t % 4, :], ctxT[:, c % 2, o:o + n], wv[:], start=True, stop=True).then_inc(valued, 1)

        @block.scalar
        def _(act):
            act.wait_ge(zer, 1)

            def transposed_chunk(c):
                k0, w = CHUNKS[c]
                act.wait_ge(transposed, c + 1)
                if c >= 2:
                    act.wait_ge(valued, 4 * (c - 1))
                    act.wait_ge(low, c - 1)
                nc.scalar.activation(ctxT[:, c % 2, 0:w], tp[:, c % 2, 0:w], ACT.Copy).then_inc(ctxT_ready, 1)

            transposed_chunk(0)
            for c in range(NC):
                for t, n in tiles_of(c):
                    act.wait_ge(valued, t + 1)
                    if t == 4 * c and c >= 2:
                        act.wait_ge(stored[c % 2], 16 * (c // 2))
                    o = (t - 4 * c) * HD1
                    nc.scalar.activation(vb[0:n, c % 2, :, o:o + HD1],
                                         vp[0:n, t % 4, :].rearrange("p (h d) -> p h d", d=HD1), ACT.Copy).then_inc(vcopied, 1)
                    if t == 4 * c and c + 1 < NC:
                        transposed_chunk(c + 1)

        @block.vector
        def _(dve):
            for c, (k0, w) in enumerate(CHUNKS):
                k = slice(k0, k0 + w)
                dve.wait_ge(ctxT_ready, c + 1)
                nc.vector.tensor_copy(cH[0:CD, k], ctxT[:, c % 2, 0:w]).then_inc(high, 1)
                nc.vector.tensor_copy(cT16[0:CD, k], ctxT[:, c % 2, 0:w])
                dve.wait_ge(high, c + 1)
                nc.vector.tensor_tensor(cL[:, k], ctxT[:, c % 2, 0:w], cH[0:CD, k].bitcast(F32), ALU.subtract).then_inc(low, 1)
    m.close()


def attention1_block(nc, A, T):
    m = Mem(nc)
    cH, cL, cT16, qH, qL, q16, O1 = T["cH"], T["cL"], T["cT16"], T["qH"], T["qL"], T["q16"], T["O1"]
    NM = NT * NC
    PER = NM + 1
    SHIFT_TILE = KT - 3
    scale = float(HD1) ** -0.5
    probs = m.sb("probs1", [P, PROB_RING, N])
    sums = m.sb("sums1", [P, N])
    cmax = m.sb("cmax1", [P, NM])
    negm = m.sb("negm1", [P, NT])
    negmT = m.sb("negmT1", [NT, P], F32R)
    rr = m.sb("rr1", [P, HALF])
    Vs = m.sb("Vs1", [P, KT, HD1])
    ones = m.sb("ones1", [P, HD1])
    sp2 = m.ps("scores1", [P, SCORE_RING, 2, HALF])
    mp = m.ps("maxps1", [P, MAX_RING0, HALF])
    acc = m.ps("acc1", [P, HALF])
    scored = m.sem("a1_scored")
    probs_ready = m.sem("a1_probs_ready")
    weighed = m.sem("a1_weighed")
    summed = m.sem("a1_summed")
    acc_copied = m.sem("a1_acc_copied")
    total_ready = m.sem("a1_total_ready")
    acc_free = m.sem("a1_acc_free")
    mscored = m.sem("a1_max_scored")
    maxed = m.sem("a1_maxed")
    negm_ready = m.sem("a1_negm_ready")
    shift_ready = m.sem("a1_shift_ready")
    shift_stored = m.sem("a1_shift_stored")
    negmT_ready = m.sem("a1_negmT_ready")
    vs_ready = [m.sem(f"a1_vs_ready{i}") for i in range(2)]
    ones_ready = m.sem("a1_ones_ready")
    recip = m.sem("a1_recip")

    def key_tile(t):
        return P if t < KF else TAIL

    def want(t):
        return min(NM, (t + 1) * NM // (SHIFT_TILE - 1) + 1)

    with nc.Block() as block:
        @block.tensor
        def _(pe):
            def max_matmul(u, n):
                q, c = divmod(n, NC)
                k0, w = CHUNKS[c]
                back = back_in_ring(n, PER, MAX_RING0)
                pe.wait_ge(maxed, PER * u + n - back + 1 + MAX_CREDIT)
                nc.tensor.matmul(mp[:, n % MAX_RING0, 0:w],
                                 q16[0:CR, ds(u, 1), q * P:(q + 1) * P].rearrange("r a q -> r (a q)"),
                                 cT16[0:CR, k0:k0 + w], start=True, stop=True).then_inc(mscored, 1)

            def shift_transpose(u):
                pe.wait_ge(negm_ready, u + 1)
                nc.tensor.transpose(mp[0:NT, NM % MAX_RING0, 0:P], negm[:], T["ident"][:]).then_inc(mscored, 1)

            def score(u, t):
                pe.wait_ge(probs_ready, KT * u + t + (2 if t == 0 else 1))
                k = slice(t * P, (t + 1) * P)
                for n, (c, q, r) in enumerate(((cH, qH, CR), (cL, qH, CD), (cH, qL, CD))):
                    for hf in range(2):
                        ins = nc.tensor.matmul(sp2[:, t % 2, hf, :], c[0:r, k],
                                               q[0:r, ds(u, 1), hf * HALF:(hf + 1) * HALF].rearrange("r a q -> r (a q)"),
                                               start=(n == 0), stop=(n == 2))
                ins.then_inc(scored, 1)

            def weigh(u, t):
                kn = key_tile(t)
                pe.wait_ge(probs_ready, KT * u + t + 1 + SCORE_RING)
                for hf in range(2):
                    ins = nc.tensor.matmul(acc[HD1 * hf:HD1 * hf + HD1, :], Vs[0:kn, t, :],
                                           probs[0:kn, t % PROB_RING, hf * HALF:(hf + 1) * HALF],
                                           start=(t == 0), stop=(t == KT - 1), skip_group_check=True)
                ins.then_inc(weighed, 1)

            def unit(u, nxt):
                pe.wait_ge(shift_ready, 16 * u + 16)
                LAG = 1
                done = 0
                for t in range(KT):
                    score(u, t)
                    if nxt is not None:
                        while done < want(t):
                            max_matmul(nxt, done)
                            done += 1
                        if t == SHIFT_TILE:
                            shift_transpose(nxt)
                    if t >= LAG:
                        if t == LAG:
                            pe.wait_ge(acc_free, u + 1)
                            pe.wait_ge(vs_ready[0], 16 * u + 16)
                        if t - LAG == MID_TILE:
                            pe.wait_ge(vs_ready[1], 16 * u + 16)
                        weigh(u, t - LAG)
                for t in range(KT - LAG, KT):
                    weigh(u, t)
                pe.wait_ge(acc_copied, u + 1)
                pe.wait_ge(summed, KT * u + KT + PROB_RING)
                for hf in range(2):
                    ins = nc.tensor.matmul(acc[HD1 * hf:HD1 * hf + HD1, :], ones[:], sums[:, hf * HALF:(hf + 1) * HALF],
                                           start=True, stop=True, skip_group_check=True)
                ins.then_inc(total_ready, 1)

            pe.sem_inc(weighed, PROB_RING)
            pe.wait_ge(ones_ready, 1)
            for n in range(NM):
                max_matmul(0, n)
            shift_transpose(0)
            with pe.Fori(0, H1 - 1) as u:
                unit(u, u + 1)
            unit(H1 - 1, None)

        @block.vector
        def _(dve):
            def maximum(u, n):
                w = CHUNKS[n % NC][1]
                dve.wait_ge(mscored, PER * u + n + 1)
                nc.vector.tensor_reduce(cmax[:, n:n + 1], mp[:, n % MAX_RING0, 0:w], AX.X, ALU.max).then_inc(maxed, 1)

            def shift(u, first):
                dve.wait_ge(maxed, PER * u + NM + MAX_CREDIT)
                nc.vector.tensor_reduce(negm[:], cmax[:].rearrange("p (q c) -> p q c", c=NC), AX.X, ALU.max,
                                        negate=True).then_inc(negm_ready, 1)
                dve.wait_ge(mscored, PER * u + NM + 1)
                if not first:
                    dve.wait_ge(shift_ready, 16 * u)
                nc.vector.tensor_copy(negmT[:], mp[0:NT, NM % MAX_RING0, 0:P]).then_inc(negmT_ready, 1)
                dve.wait_ge(negmT_ready, u + 1)
                dve.sem_inc(maxed, 1)

            def add_up(u, t):
                kn = key_tile(t)
                pr = probs[0:kn, t % PROB_RING, :]
                dve.wait_ge(probs_ready, KT * u + t + 1 + SCORE_RING)
                dve.wait_ge(summed, KT * u + t + PROB_RING)
                if t == 0:
                    ins = nc.vector.tensor_copy(sums[:], pr)
                else:
                    ins = nc.vector.tensor_tensor(sums[0:kn, :], sums[0:kn, :], pr, ALU.add)
                ins.then_inc(summed, 1)

            def unit(u, nxt):
                done = 0
                for t in range(KT):
                    if nxt is not None:
                        while done < want(t):
                            maximum(nxt, done)
                            done += 1
                        if t == SHIFT_TILE:
                            shift(nxt, False)
                    add_up(u, t)
                dve.wait_ge(total_ready, u + 1)
                nc.vector.reciprocal(rr[:], acc[:]).then_inc(acc_free, 1)
                dve.wait_ge(acc_free, u + 2)
                dve.wait_ge(acc_copied, u + 1)
                o = O1[:, ds(u, 1), :].rearrange("p a q -> p (a q)")
                nc.vector.tensor_tensor(o, o, rr[:], ALU.mult).then_inc(recip, 1)
                dve.wait_ge(recip, u + 1)

            nc.vector.memset(ones[:], 1.0).then_inc(ones_ready, 1)
            dve.sem_inc(maxed, MAX_CREDIT)
            dve.sem_inc(summed, PROB_RING)
            dve.sem_inc(acc_free, 1)
            for n in range(NM):
                maximum(0, n)
            shift(0, True)
            with dve.Fori(0, H1 - 1) as u:
                unit(u, u + 1)
            unit(H1 - 1, None)

        @block.scalar
        def _(act):
            act.sem_inc(probs_ready, SCORE_RING)
            with act.Fori(0, H1) as u:
                for t in range(KT):
                    kn = key_tile(t)
                    act.wait_ge(scored, KT * u + t + 1)
                    act.wait_ge(weighed, KT * u + t + 1)
                    act.wait_ge(summed, KT * u + t + 1)
                    nc.scalar.activation(probs[0:kn, t % PROB_RING, :],
                                         sp2[0:kn, t % 2, :, :].rearrange("p i q -> p (i q)"), ACT.Exp,
                                         scale=scale).then_inc(probs_ready, 1)
                act.wait_ge(weighed, KT * u + KT + PROB_RING)
                nc.scalar.activation(O1[:, ds(u, 1), :].rearrange("p a q -> p (a q)"), acc[:], ACT.Copy).then_inc(acc_copied, 1)

        @block.gpsimd
        def _(pool):
            def stage(u, part):
                t0, t1 = ((0, MID_TILE), (MID_TILE, KT))[part]
                src = T["v1_dram"][ds(u, 1), :, t0:t1, :].rearrange("a p t d -> (a p) t d")
                pool.dma_start(Vs[:, t0:t1, :], src).then_inc(vs_ready[part], 16)

            stage(0, 0)
            stage(0, 1)
            with pool.Fori(1, H1) as u:
                for part, t1 in enumerate((MID_TILE, KT)):
                    pool.wait_ge(weighed, KT * u - KT + t1 + PROB_RING)
                    stage(u, part)

        @block.sync
        def _(sp):
            with sp.Fori(0, H1) as u:
                sp.wait_ge(negmT_ready, u + 1)
                sp.dma_start(T["shift1_dram"][ds(u, 1), :].rearrange("a (j p) -> (a j) p", p=P), negmT[:].bitcast(F32)).then_inc(shift_stored, 16)
                sp.wait_ge(shift_stored, 16 * u + 16)
                sp.dma_start(qH[CD:CD + 1, ds(u, 1), :].bitcast(F32), T["shift1_dram"][ds(u, 1), :].unsqueeze(0)).then_inc(shift_ready, 16)
    m.close()


def project1_block(nc, A, T):
    m = Mem(nc)
    O1, x = T["O1"], T["x"]
    bo = m.sb("bo1", [P, D])
    wo = m.sb("wo1", [P, H1, D])
    tot = m.sb("tot1", [P, NT, D])
    yp = m.ps("yp1", [P, 2, 4, D])
    loaded = m.sem("p1_loaded")
    projected = m.sem("p1_projected")
    added = m.sem("p1_added")
    with nc.Block() as block:
        @block.sync
        def _(sp):
            sp.dma_start(bo[:], A["L1_xattn_b_o"].partition_broadcast(P)).then_inc(loaded, 16)
            for f in range(2):
                sp.dma_start(wo[HD1 * f:HD1 * f + HD1, :, :], A["L1_xattn_W_o"].rearrange("(h d) n -> d h n", d=HD1)).then_inc(loaded, 16)

        @block.tensor
        def _(pe):
            pe.wait_ge(loaded, 48)
            for f in range(2):
                r = slice(HD1 * f, HD1 * f + HD1)
                for i in range(4):
                    for h in range(H1):
                        last = nc.tensor.matmul(yp[:, f, i, :], O1[r, h, i * P:(i + 1) * P], wo[r, h, :],
                                                start=(h == 0), stop=(h == H1 - 1))
                last.then_inc(projected, 1)

        @block.vector
        def _(dve):
            for f in range(2):
                i = slice(4 * f, 4 * f + 4)
                dve.wait_ge(projected, f + 1)
                nc.vector.tensor_tensor(tot[:, i, :], yp[:, f, :, :], bo[:].unsqueeze(1).broadcast_to([P, 4, D]), ALU.add).then_inc(added, 1)
                dve.wait_ge(added, f + 1)
                nc.vector.scalar_tensor_tensor(out=x[:, i, :], in0=tot[:, i, :], scalar=T["tg"][:, 1:2], in1=x[:, i, :],
                                               op0=ALU.mult, op1=ALU.add)
    m.close()


def rope_block(nc, A, T):
    m = Mem(nc)
    w = m.sb("w_qkv", [P, 3 * D])
    cs = m.sb("cos_sin", [P, 2, NT, HD0 // 2])
    qkv = m.sb("qkv", [P, NT, 3 * D])
    rot = m.sb("rot", [P, NT, 2 * D])
    tt = m.sb("rope_terms", [P, 4, NT, 2 * H0, HD0 // 2])
    pp = m.ps("qkv_ps", [P, 2, HALF])
    tp = m.ps("rot_tp", [P, 2, NT, P])
    loaded = m.sem("r_loaded")
    projected = m.sem("r_projected")
    copied = m.sem("r_copied")
    own = m.sem("r_vector_chain")
    turned = m.sem("r_turned")
    transposed = m.sem("r_transposed")
    with nc.Block() as block:
        @block.sync
        def _(sp):
            sp.dma_start(w[:], A["L1_ffn_w_qkv"]).then_inc(loaded, 16)
            sp.dma_start(cs[:], A["cos_sin"].rearrange("s (i p) d -> p s i d", p=P)).then_inc(loaded, 16)

        @block.tensor
        def _(pe):
            pe.wait_ge(loaded, 32)
            for i in range(NT):
                if i >= 2:
                    pe.wait_ge(copied, i - 1)
                nc.tensor.matmul(pp[:, i % 2, 0:3 * D], T["xT"][:, i * P:(i + 1) * P], w[:], start=True, stop=True).then_inc(projected, 1)
            pe.wait_ge(turned, 2)
            for s in range(2):
                for i in range(NT):
                    last = nc.tensor.transpose(tp[:, s, i, :], rot[:, i, s * D:(s + 1) * D], T["ident"][:])
                last.then_inc(transposed, 1)

        @block.scalar
        def _(act):
            for i in range(NT):
                act.wait_ge(projected, i + 1)
                nc.scalar.activation(qkv[:, i, :], pp[:, i % 2, 0:3 * D], ACT.Copy).then_inc(copied, 1)
            for s, dst in enumerate((T["qT"], T["kT"])):
                act.wait_ge(transposed, s + 1)
                for b in range(2):
                    nc.scalar.activation(dst[:, b * HALF:(b + 1) * HALF], tp[:, s, 4 * b:4 * b + 4, :], ACT.Copy)

        @block.vector
        def _(dve):
            chain = Chain(dve, own)
            dve.wait_ge(loaded, 32)
            dve.wait_ge(copied, NT)
            nc.vector.tensor_copy(T["V2"][:, :, :, 0:HD0], qkv[:, :, 2 * D:3 * D].rearrange("p i (h d) -> p i h d", d=HD0))
            x = qkv[:, :, 0:2 * D].rearrange("p i (h k e) -> p i h k e", k=HD0 // 2, e=2)
            o = rot[:, :, :].rearrange("p i (h k e) -> p i h k e", k=HD0 // 2, e=2)
            for n, (e, f) in enumerate(((0, 0), (1, 1), (0, 1), (1, 0))):
                for i in range(NT):
                    last = nc.vector.tensor_tensor(tt[:, n, i], x[:, i, :, :, e],
                                                   cs[:, f, i, :].unsqueeze(1).broadcast_to([P, 2 * H0, HD0 // 2]), ALU.mult)
            chain.link(last)
            for i in range(NT):
                nc.vector.tensor_tensor(o[:, i, :, :, 0], tt[:, 0, i], tt[:, 1, i], ALU.subtract)
                last = nc.vector.tensor_tensor(o[:, i, :, :, 1], tt[:, 2, i], tt[:, 3, i], ALU.add)
            last.then_inc(turned, 2)

        @block.gpsimd
        def _(pool):
            nc.gpsimd.memset(T["V2"][:, :, :, HD0:VW], 1.0)
    m.close()


def self_block(nc, A, T):
    m = Mem(nc)
    K2, Q2, V2, Oraw = T["K2"], T["Q2"], T["V2"], T["Oraw"]
    scale = float(HD0) ** -0.5
    RING = 4
    probs = m.sb("probs2", [P, RING, 2, HALF])
    cmax = m.sb("cmax2", [P, 2, 16, 2])
    negm = m.sb("negm2", [P, 2, 16])
    negmT = m.sb("negmT2", [16, 2, P], BF16)
    zeros = m.sb("zeros2", [P, HALF])
    tri = m.sb("tri", [P, 2, P], BF16)
    sp2 = m.ps("scores2", [P, 2, 2, HALF])
    mp = m.ps("maxps2", [P, 3, HALF])
    acc = m.ps("acc2", [P, HALF])
    loaded = m.sem("s_loaded")
    zer = m.sem("s_zeroed")
    scored = m.sem("s_scored")
    probs_ready = m.sem("s_probs_ready")
    weighed = m.sem("s_weighed")
    acc_free = m.sem("s_acc_free")
    mscored = m.sem("s_max_scored")
    maxed = m.sem("s_maxed")
    negm_ready = m.sem("s_negm_ready")
    negmT_ready = m.sem("s_negmT_ready")
    shift_ready = [m.sem(f"s_shift_ready{i}") for i in range(2)]
    shift_stored = m.sem("s_shift_stored")

    def entries(f):
        out = []
        for q in range(16):
            i = 4 * f + q % 4
            if i < 4:
                out.append((q, 0, (i + 1) * P, True, 0))
            else:
                out.append((q, 0, HALF, False, 0))
                out.append((q, HALF, (i - 3) * P, True, 1))
        return out + [None]

    ENT = [(u, e) for u in range(NU0) for e in entries(u % 2)]
    first = [next(n for n, (v, _) in enumerate(ENT) if v == u) for u in range(NU0)] + [len(ENT)]
    PAIR = [(u, t, b) for u in range(NU0) for t in range(4 * (u % 2) + 4) for b in range(2)]

    with nc.Block() as block:
        @block.sync
        def _(sp):
            sp.dma_start(tri[:], A["tri16"].rearrange("s p q -> p s q")).then_inc(loaded, 16)
            for u in range(NU0):
                sp.wait_ge(negmT_ready, u + 1)
                sp.dma_start(T["shift2_dram"][u].rearrange("(j p) -> j p", p=P), negmT[:, u % 2, :]).then_inc(shift_stored, 16)
                sp.wait_ge(shift_stored, 16 * u + 16)
                sp.dma_start(Q2[0:1, u, :], T["shift2_dram"][u:u + 1, :]).then_inc(shift_ready[u % 2], 16)

        @block.tensor
        def _(pe):
            def entry(n):
                u, e = ENT[n]
                bank = n % 3
                if n >= 3:
                    pe.wait_ge(maxed, n - 2)
                if e is None:
                    pe.wait_ge(negm_ready, u + 1)
                    nc.tensor.transpose(mp[0:16, bank, 0:P], negm[:, u % 2, :], T["ident"][:]).then_inc(mscored, 1)
                    return
                q, k0, w, diag, _ = e
                ins = nc.tensor.matmul(mp[:, bank, 0:w], Q2[0:ROWS, u, q * P:(q + 1) * P],
                                       K2[0:ROWS, u // 2 * 2 + q // 8, k0:k0 + w], start=True, stop=True)
                if diag:
                    ins = nc.tensor.matmul(mp[:, bank, w - P:w], T["ident16"][:], tri[:, 0, :], start=False, stop=True,
                                           skip_group_check=True)
                ins.then_inc(mscored, 1)

            def score(n):
                u, t, b = PAIR[n]
                f = u % 2
                c0 = max(0, t - 4 * f) * P
                if n >= 2:
                    pe.wait_ge(probs_ready, n - 1)
                for i in range(2):
                    j = 2 * b + i
                    ins = nc.tensor.matmul(sp2[:, n % 2, i, c0:HALF], K2[0:ROWS, u // 2 * 2 + b, t * P:(t + 1) * P],
                                           Q2[0:ROWS, u, j * HALF + c0:(j + 1) * HALF], start=True, stop=True)
                    if t >= 4 * f:
                        ins = nc.tensor.matmul(sp2[:, n % 2, i, c0:c0 + P], T["ident16"][:], tri[:, 1, :],
                                               start=False, stop=True, skip_group_check=True)
                ins.then_inc(scored, 1)

            def weigh(n):
                u, t, _ = PAIR[n]
                f = u % 2
                c0 = max(0, t - 4 * f) * P
                if t == 0 and u >= 1:
                    pe.wait_ge(acc_free, u)
                pe.wait_ge(probs_ready, n + 1)
                for j in range(GH):
                    ins = nc.tensor.matmul(acc[32 * j:32 * j + VW, c0:HALF], V2[:, t, 4 * (u // 2) + j, :],
                                           probs[:, (n - 1 + j // 2) % RING, j % 2, c0:HALF], start=(t == 0), stop=(t == 4 * f + 3),
                                           skip_group_check=True)
                ins.then_inc(weighed, 2)

            pe.wait_ge(loaded, 16)
            pe.wait_ge(zer, 1)
            nc.tensor.matmul(acc[:], zeros[:, 0:P], zeros[:], start=True, stop=True)
            lead = first[1] + 20
            for n in range(lead):
                entry(n)
            n = lead
            for k, (u, t, b) in enumerate(PAIR):
                if (t, b) == (0, 0):
                    pe.wait_ge(shift_ready[u % 2], 16 * (u // 2 + 1))
                score(k)
                while n < min(len(ENT), lead + (k + 1) * (len(ENT) - lead) // (len(PAIR) - 26)):
                    entry(n)
                    n += 1
                if t >= 1 and b == 1:
                    weigh(k - 2)
                if k + 1 == len(PAIR) or PAIR[k + 1][0] != u:
                    weigh(k)

        @block.vector
        def _(dve):
            nc.vector.memset(zeros[:], 0.0).then_inc(zer, 1)
            for n, (u, e) in enumerate(ENT):
                bank = n % 3
                if e is None:
                    dve.wait_ge(maxed, n)
                    if u % 2:
                        src = cmax[:, 1, :, :]
                    else:
                        src = cmax[:, 0, :, 0:1]
                    if u >= 2:
                        dve.wait_ge(mscored, first[u - 1])
                    nc.vector.tensor_reduce(negm[:, u % 2, :], src, AX.X, ALU.max, negate=True).then_inc(negm_ready, 1)
                    dve.wait_ge(mscored, n + 1)
                    if u >= 2:
                        dve.wait_ge(shift_ready[u % 2], 16 * (u // 2))
                    nc.vector.tensor_copy(negmT[:, u % 2, :], mp[0:16, bank, 0:P]).then_inc(negmT_ready, 1)
                    dve.wait_ge(negmT_ready, u + 1)
                    dve.sem_inc(maxed, 1)
                    continue
                q, k0, w, diag, c = e
                dve.wait_ge(mscored, n + 1)
                nc.vector.tensor_reduce(cmax[:, u % 2, q, c:c + 1], mp[:, bank, 0:w], AX.X, ALU.max).then_inc(maxed, 1)

        @block.scalar
        def _(act):
            for n, (u, t, b) in enumerate(PAIR):
                c0 = max(0, t - 4 * (u % 2)) * P
                act.wait_ge(scored, n + 1)
                if n >= RING:
                    act.wait_ge(weighed, n - RING + 1)
                nc.scalar.activation(probs[:, n % RING, :, c0:HALF], sp2[:, n % 2, :, c0:HALF], ACT.Exp,
                                     scale=scale).then_inc(probs_ready, 1)
                if n + 1 == len(PAIR) or PAIR[n + 1][0] != u:
                    act.wait_ge(weighed, n + 1)
                    nc.scalar.activation(Oraw[:, u, :], acc[:], ACT.Copy).then_inc(acc_free, 1)
    m.close()


def store_block(nc, src, dst, T):
    m = Mem(nc)
    stored = m.sem("out_stored")
    with nc.Block() as block:
        @block.sync
        def _(sp):
            sp.dma_start(dst[0].rearrange("(i p) d -> p i d", p=P), src[:]).then_inc(stored, 16)
            sp.wait_ge(stored, 16)
    m.close()


def gated_blocks(nc: bass.Bass, A, out):
    T = {}
    m = Mem(nc)
    T["k0_dram"] = nc.dram_tensor("k0_parts_dram", (3, D, CTX), BF16).ap()
    T["q_dram"] = nc.dram_tensor("q_parts_dram", (3, D, N), BF16).ap()
    T["ks_dram"] = nc.dram_tensor("ks_parts_dram", (3, D, N), BF16).ap()
    T["shift0_dram"] = nc.dram_tensor("shift0_dram", (NU0, 2 * N), BF16).ap()
    T["shift1_dram"] = nc.dram_tensor("shift1_dram", (H1, N), F32).ap()
    T["shift2_dram"] = nc.dram_tensor("shift2_dram", (NU0, 2 * N), BF16).ap()
    T["pen16_dram"] = nc.dram_tensor("pen16_dram", (2, KT * P), BF16).ap()
    T["rows32_dram"] = nc.dram_tensor("rows32_dram", (2, KT * P), F32).ap()
    T["v1_dram"] = nc.dram_tensor("v1_dram", (H1, P, KT, HD1), F32).ap()
    for name, shape, dt in (("x", [P, NT, D], F32), ("ident", [P, P], F32), ("ident16", [P, P], BF16),
                            ("g", [P, 4], F32), ("tg", [P, 4], F32), ("any", [P, 2], F32), ("iota8", [P, 8], F32)):
        T[name] = m.sb(name, shape, dt)
    load_block(nc, A, T)
    x = T["x"]

    m0 = Mem(nc)
    T["K2"] = m0.sb("K2", [P, H0 // 2, CTX], BF16)
    T["Q2"] = m0.sb("Q2", [P, NU0, 2 * N], BF16)
    T["V0"] = m0.sb("V0", [P, KT, H0, HD0])
    T["Vs"] = m0.sb("Vs", [P, KT, GH, VW])
    context0_block(nc, A, T)
    m1 = Mem(nc)
    xn, xT = m1.sb("xn0", [P, NT, D]), m1.sb("xT0", [P, N])
    norm_block(nc, "ln0", x, xn, xT, T["ident"], EPS_LN)
    operand_block(nc, "q0", A, T, A["L0_xattn_Wq"], xT, None, T["any"][:, 0:1])
    m1.close()
    T["Oraw"] = m0.sb("Oraw0", [P, NU0, HALF])
    attention0_block(nc, A, T)
    project_block(nc, "o0", A, T, T["Oraw"], A["L0_xattn_Wo"], x, x, T["tg"][:, 0:1])
    m0.close()

    m0 = Mem(nc)
    xn, xT, comb = m0.sb("xn1", [P, NT, D]), m0.sb("xT1", [P, N]), m0.sb("comb0", [P, NT, 8])
    norm_block(nc, "ln1", x, xn, xT, T["ident"], EPS_LN)
    gate_block(nc, "g0", A, T, xT, A["L0_ffn_gate_w"], comb, 0)
    experts_block(nc, "e0", A, T, xT, comb, A["L0_ffn_w1"], A["L0_ffn_b1"], A["L0_ffn_w2"], A["L0_ffn_b2"],
                  A["L0_ffn_w1"].shape[2], ACT.Gelu, x, x, T["tg"][:, 2:3], None)
    m0.close()

    m0 = Mem(nc)
    for name, shape, dt in (("cH", [CR, KT * P], F32R), ("cL", [CD, KT * P], F32R), ("cT16", [CR, CTX], BF16),
                            ("qH", [CR, H1, N], F32R), ("qL", [CD, H1, N], F32R), ("q16", [CR, H1, N], BF16)):
        T[name] = m0.sb(name, shape, dt)
    m1 = Mem(nc)
    xn, T["xT"] = m1.sb("xn2", [P, NT, D]), m1.sb("xT2", [P, N])
    norm_block(nc, "ln2", x, xn, T["xT"], T["ident"], EPS_LN)
    query1_block(nc, A, T)
    m1.close()
    context1_block(nc, A, T)
    T["O1"] = m0.sb("O1", [P, H1, HALF])
    attention1_block(nc, A, T)
    project1_block(nc, A, T)
    m0.close()

    m0 = Mem(nc)
    gains = m0.sb("gains", [P, 2, D])
    xin, xn, T["xT"] = m0.sb("xin", [P, NT, D]), m0.sb("xn3", [P, NT, D]), m0.sb("xT3", [P, N])
    norm_block(nc, "ln3", x, xin, T["xT"], T["ident"], EPS_LN)
    gl = m0.sem("gains_loaded")
    with nc.Block() as block:
        @block.sync
        def _(sp):
            sp.dma_start(gains[:, 0, :], A["L1_ffn_g1"].partition_broadcast(P)).then_inc(gl, 16)
            sp.dma_start(gains[:, 1, :], A["L1_ffn_g2"].partition_broadcast(P)).then_inc(gl, 16)
            sp.wait_ge(gl, 32)
    norm_block(nc, "rms1", xin, xn, T["xT"], T["ident"], EPS_RMS, gains[:, 0, :])
    m1 = Mem(nc)
    T["V2"] = m1.sb("V2", [P, NT, H0, VW])
    T["K2"] = m1.sb("K2b", [P, H0 // 2, N], BF16)
    T["Q2"] = m1.sb("Q2b", [P, NU0, 2 * N], BF16)
    T["qT"], T["kT"] = m1.sb("qT", [P, N]), m1.sb("kT", [P, N])
    rope_block(nc, A, T)
    operand_block(nc, "q2", A, T, None, T["qT"], T["kT"], None)
    T["Oraw"] = m1.sb("Oraw2", [P, NU0, HALF])
    self_block(nc, A, T)
    project_block(nc, "o2", A, T, T["Oraw"], A["L1_ffn_w_o"], xin, xin, None)
    m1.close()
    comb = m0.sb("comb1", [P, NT, 8])
    res = m0.sb("res", [P, NT, D])
    norm_block(nc, "rms2", xin, xn, T["xT"], T["ident"], EPS_RMS, gains[:, 1, :])
    gate_block(nc, "g1", A, T, T["xT"], A["L1_ffn_w_router"], comb, MOE_CAP)
    experts_block(nc, "e1", A, T, T["xT"], comb, A["L1_ffn_w1"], None, A["L1_ffn_w2"], None,
                  A["L1_ffn_w1"].shape[2], ACT.Relu, res, x, T["tg"][:, 3:4], xin)
    store_block(nc, res, out, T)
    m0.close()
    m.close()


MOE_CAP = -(-2 * 256 * 2 * 5 // (4 * 8))


def constants():
    half = HD0 // 2
    theta = (np.float32(10000.0) ** (np.float32(-2.0) * (np.arange(half, dtype=np.float32) / np.float32(HD0)))).astype(np.float32)
    ang = np.arange(N, dtype=np.float32)[:, None] * theta[None, :]
    sumpick = np.zeros((P, NU0, 32), np.float32)
    sumspread = np.zeros((P, NU0, P), np.float32)
    for u in range(NU0):
        for j in range(GH):
            r = 16 * (u // 4) + 4 * j
            sumpick[32 * j + HD0, u, r:r + 4] = 1.0
            sumspread[32 * (u % 4) + r, u, 32 * j:32 * j + 32] = 1.0
    later = np.triu(np.full((P, P), -BIG, np.float32), 1)
    return {
        "ident": np.eye(P, dtype=np.float32),
        "ident16": np.eye(P, dtype=np.float32),
        "ones16": np.ones((1, CTX), np.float32),
        "ones32": np.ones((1, KT * P), np.float32),
        "sumpick": sumpick,
        "sumspread": sumspread,
        "tri16": np.stack([later, later.T]),
        "iota8": np.arange(8, dtype=np.float32),
        "cos_sin": np.stack([np.cos(ang), np.sin(ang)]).astype(np.float32),
    }


def kernel(**inputs):
    import concourse.bacc as bacc
    from concourse.bass_utils import run_bass_kernel_spmd

    nc = bacc.Bacc("TRN2", target_bir_lowering=False, num_devices=1)
    arrays, A = {}, {}

    def give(name, a):
        a = np.ascontiguousarray(a)
        arrays[f"in_{name}"] = a
        return nc.dram_tensor(f"in_{name}", a.shape, mybir.dt.from_np(a.dtype), kind="ExternalInput").ap()

    for name, a in inputs.items():
        a = np.asarray(a)
        if a.dtype == np.bool_:
            A[name] = give(name, a.view(np.uint32)).bitcast(U8)
        else:
            A[name] = give(name, a)
    for name, a in constants().items():
        if name.endswith("16"):
            A[name] = give(name, (a.view(np.uint32) >> 16).astype(np.uint16)).bitcast(BF16)
        else:
            A[name] = give(name, a)
    A["ctx"] = A["ctx_768"]
    A["masks"] = (A["mask_BxS2_bf1"], A["mask_BxS2_bk0"])
    out = nc.dram_tensor("out_dram", (1, N, D), F32, kind="ExternalOutput").ap()
    gated_blocks(nc, A, out)
    r = run_bass_kernel_spmd(nc, [arrays], core_ids=[0])
    return r.results[0]["out_dram"]
```
